# Optimizing a Trainium2 kernel written in Bass

```python
import numpy as np
import jax
import jax.numpy as jnp

def _softmax(x, axis=-1):
    return jax.nn.softmax(x, axis=axis)

def _gelu(x):
    return jax.nn.gelu(x, approximate=True)

def _silu(x):
    return jax.nn.silu(x)

def _sigmoid(x):
    return jax.nn.sigmoid(x)

def _layernorm(x, axis=-1, eps=1e-05):
    m = jnp.mean(x, axis=axis, keepdims=True)
    v = jnp.var(x, axis=axis, keepdims=True)
    return (x - m) / jnp.sqrt(v + eps)

def _scatter_add(tgt, idx, src, axis=0):
    return tgt.at[idx].add(src)

def _segment_sum(src, seg, n):
    return jax.ops.segment_sum(src, seg, n)
kernel_name = 'mk_seq_preln_d1_jaxref_r8_396c38'

def setup_inputs(seed: int=0):
    np.random.seed(seed)
    _w = jnp.asarray

    def _L0_attn_setup():
        import jax, jax.numpy as jnp
        import numpy as np
        D = 128
        I = 256
        NH = 4
        DH = I // NH
        QKB = 4
        NQK = I // QKB
        E = 8
        TOPK = 2
        B = 4
        S = 256
        LN_EPS = 1e-05
        CELL_EPS = 1e-06

        def _layernorm(x, w):
            mu = jnp.mean(x, -1, keepdims=True)
            var = jnp.mean(jnp.square(x - mu), -1, keepdims=True)
            return (x - mu) * jax.lax.rsqrt(var + LN_EPS) * w

        def _headwise(x, w):
            h = x.reshape(-1, NQK, QKB)
            return jnp.einsum('tnb,nob->tno', h, w).reshape(-1, I)

        def _expert(x, ln_w, w_up, conv_w, conv_b, q_w, k_w, v_w, ig_w, ig_b, on_w, skip_w, w_down):
            xn = _layernorm(x, ln_w)
            up = xn @ w_up
            x_m, z = (up[:, :I], up[:, I:])
            conv = x_m * conv_w[:, -1] + conv_b
            conv_act = conv * jax.nn.sigmoid(conv)
            q = _headwise(conv_act, q_w)
            k = _headwise(conv_act, k_w)
            v = _headwise(x_m, v_w)
            ig = jnp.concatenate([q, k, v], -1) @ ig_w + ig_b
            qh = q.reshape(-1, NH, DH)
            kh = k.reshape(-1, NH, DH)
            vh = v.reshape(-1, NH, DH)
            qk = jnp.sum(qh * kh, -1) * DH ** (-0.5)
            normalizer = jnp.maximum(jnp.abs(qk), jnp.exp(-ig))
            h = (qk / (normalizer + CELL_EPS))[..., None] * vh
            mu = jnp.mean(h, -1, keepdims=True)
            var = jnp.mean(jnp.square(h - mu), -1, keepdims=True)
            hn = ((h - mu) * jax.lax.rsqrt(var + LN_EPS)).reshape(-1, I) * on_w
            hs = (hn + skip_w * conv_act) * jax.nn.silu(z)
            return x + hs @ w_down

        def _reference_tuple_inner(hidden_states, gate_w, ln_w, w_up, conv_w, conv_b, q_w, k_w, v_w, ig_w, ig_b, fg_w, fg_b, on_w, skip_w, w_down):
            Bz, Sq, Dm = hidden_states.shape
            flat = hidden_states.reshape(-1, Dm)
            router_logits = flat @ gate_w
            rw = jax.nn.softmax(router_logits, -1)
            top_w, top_i = jax.lax.top_k(rw, TOPK)
            top_w = top_w / jnp.sum(top_w, -1, keepdims=True)
            out = jnp.zeros_like(flat)
            for e in range(E):
                we = jnp.sum(jnp.where(top_i == e, top_w, 0.0), -1)
                ye = _expert(flat, ln_w[e], w_up[e], conv_w[e], conv_b[e], q_w[e], k_w[e], v_w[e], ig_w[e], ig_b[e], on_w[e], skip_w[e], w_down[e])
                out = out + we[:, None] * ye
            return (out.reshape(Bz, Sq, Dm), router_logits)
        key = jax.random.key(seed)
        ks = jax.random.split(key, 12)
        rn = lambda k, sh, sc=0.02: jax.random.normal(k, sh, dtype=jnp.float32) * sc
        return {'hidden_states': jax.random.normal(ks[0], (B, S, D), jnp.float32), 'gate_w': rn(ks[1], (D, E)), 'ln_w': jnp.ones((E, D), jnp.float32), 'w_up': rn(ks[2], (E, D, 2 * I)), 'conv_w': rn(ks[3], (E, I, 4), 0.1), 'conv_b': jnp.zeros((E, I), jnp.float32), 'q_w': rn(ks[4], (E, NQK, QKB, QKB), 0.3), 'k_w': rn(ks[5], (E, NQK, QKB, QKB), 0.3), 'v_w': rn(ks[6], (E, NQK, QKB, QKB), 0.3), 'ig_w': rn(ks[7], (E, 3 * I, NH)), 'ig_b': jnp.zeros((E, NH), jnp.float32), 'fg_w': rn(ks[8], (E, 3 * I, NH)), 'fg_b': jnp.zeros((E, NH), jnp.float32), 'on_w': jnp.ones((E, I), jnp.float32), 'skip_w': jnp.ones((E, I), jnp.float32), 'w_down': rn(ks[9], (E, I, D))}
    _L0_attn_in = _L0_attn_setup()

    def _L0_ffn_setup():
        import jax, jax.numpy as jnp
        import numpy as np
        TOP_K = 2
        key = jax.random.key(seed)
        k0, k1, k2, k3, k4 = jax.random.split(key, 5)
        B, S, D, H, E = (4, 256, 128, 256, 8)
        x = jax.random.normal(k0, (B, S, D), dtype=jnp.float32)
        router_w = jax.random.normal(k1, (E, D), dtype=jnp.float32) * D ** (-0.5)
        w_gate = jax.random.normal(k2, (E, D, H), dtype=jnp.float32) * D ** (-0.5)
        w_up = jax.random.normal(k3, (E, D, H), dtype=jnp.float32) * D ** (-0.5)
        w_down = jax.random.normal(k4, (E, H, D), dtype=jnp.float32) * H ** (-0.5)
        return {'x': x, 'router_w': router_w, 'w_gate': w_gate, 'w_up': w_up, 'w_down': w_down}
    _L0_ffn_in = _L0_ffn_setup()
    _d = {'L0_attn_hidden_states': _L0_attn_in['hidden_states'], 'L0_attn_gate_w': _L0_attn_in['gate_w'], 'L0_attn_ln_w': _L0_attn_in['ln_w'], 'L0_attn_w_up': _L0_attn_in['w_up'], 'L0_attn_conv_w': _L0_attn_in['conv_w'], 'L0_attn_conv_b': _L0_attn_in['conv_b'], 'L0_attn_q_w': _L0_attn_in['q_w'], 'L0_attn_k_w': _L0_attn_in['k_w'], 'L0_attn_v_w': _L0_attn_in['v_w'], 'L0_attn_ig_w': _L0_attn_in['ig_w'], 'L0_attn_ig_b': _L0_attn_in['ig_b'], 'L0_attn_fg_w': _L0_attn_in['fg_w'], 'L0_attn_fg_b': _L0_attn_in['fg_b'], 'L0_attn_on_w': _L0_attn_in['on_w'], 'L0_attn_skip_w': _L0_attn_in['skip_w'], 'L0_attn_w_down': _L0_attn_in['w_down'], 'L0_ffn_router_w': _L0_ffn_in['router_w'], 'L0_ffn_w_gate': _L0_ffn_in['w_gate'], 'L0_ffn_w_up': _L0_ffn_in['w_up'], 'L0_ffn_w_down': _L0_ffn_in['w_down']}
    _x0 = _d['L0_attn_hidden_states']
    _d['L0_attn_hidden_states'] = jax.random.normal(jax.random.fold_in(jax.random.key(seed), 1), (8, 256, 128), dtype=_x0.dtype)
    del _x0
    return _d

def reference(L0_attn_hidden_states, L0_attn_gate_w, L0_attn_ln_w, L0_attn_w_up, L0_attn_conv_w, L0_attn_conv_b, L0_attn_q_w, L0_attn_k_w, L0_attn_v_w, L0_attn_ig_w, L0_attn_ig_b, L0_attn_fg_w, L0_attn_fg_b, L0_attn_on_w, L0_attn_skip_w, L0_attn_w_down, L0_ffn_router_w, L0_ffn_w_gate, L0_ffn_w_up, L0_ffn_w_down):

    def _L0_attn_ref(hidden_states, gate_w, ln_w, w_up, conv_w, conv_b, q_w, k_w, v_w, ig_w, ig_b, fg_w, fg_b, on_w, skip_w, w_down):
        import jax, jax.numpy as jnp
        import numpy as np
        D = 128
        I = 256
        NH = 4
        DH = I // NH
        QKB = 4
        NQK = I // QKB
        E = 8
        TOPK = 2
        B = 4
        S = 256
        LN_EPS = 1e-05
        CELL_EPS = 1e-06

        def _layernorm(x, w):
            mu = jnp.mean(x, -1, keepdims=True)
            var = jnp.mean(jnp.square(x - mu), -1, keepdims=True)
            return (x - mu) * jax.lax.rsqrt(var + LN_EPS) * w

        def _headwise(x, w):
            h = x.reshape(-1, NQK, QKB)
            return jnp.einsum('tnb,nob->tno', h, w).reshape(-1, I)

        def _expert(x, ln_w, w_up, conv_w, conv_b, q_w, k_w, v_w, ig_w, ig_b, on_w, skip_w, w_down):
            xn = _layernorm(x, ln_w)
            up = xn @ w_up
            x_m, z = (up[:, :I], up[:, I:])
            conv = x_m * conv_w[:, -1] + conv_b
            conv_act = conv * jax.nn.sigmoid(conv)
            q = _headwise(conv_act, q_w)
            k = _headwise(conv_act, k_w)
            v = _headwise(x_m, v_w)
            ig = jnp.concatenate([q, k, v], -1) @ ig_w + ig_b
            qh = q.reshape(-1, NH, DH)
            kh = k.reshape(-1, NH, DH)
            vh = v.reshape(-1, NH, DH)
            qk = jnp.sum(qh * kh, -1) * DH ** (-0.5)
            normalizer = jnp.maximum(jnp.abs(qk), jnp.exp(-ig))
            h = (qk / (normalizer + CELL_EPS))[..., None] * vh
            mu = jnp.mean(h, -1, keepdims=True)
            var = jnp.mean(jnp.square(h - mu), -1, keepdims=True)
            hn = ((h - mu) * jax.lax.rsqrt(var + LN_EPS)).reshape(-1, I) * on_w
            hs = (hn + skip_w * conv_act) * jax.nn.silu(z)
            return x + hs @ w_down

        def _reference_tuple_inner(hidden_states, gate_w, ln_w, w_up, conv_w, conv_b, q_w, k_w, v_w, ig_w, ig_b, fg_w, fg_b, on_w, skip_w, w_down):
            Bz, Sq, Dm = hidden_states.shape
            flat = hidden_states.reshape(-1, Dm)
            router_logits = flat @ gate_w
            rw = jax.nn.softmax(router_logits, -1)
            top_w, top_i = jax.lax.top_k(rw, TOPK)
            top_w = top_w / jnp.sum(top_w, -1, keepdims=True)
            out = jnp.zeros_like(flat)
            for e in range(E):
                we = jnp.sum(jnp.where(top_i == e, top_w, 0.0), -1)
                ye = _expert(flat, ln_w[e], w_up[e], conv_w[e], conv_b[e], q_w[e], k_w[e], v_w[e], ig_w[e], ig_b[e], on_w[e], skip_w[e], w_down[e])
                out = out + we[:, None] * ye
            return (out.reshape(Bz, Sq, Dm), router_logits)
        return _reference_tuple_inner(hidden_states, gate_w, ln_w, w_up, conv_w, conv_b, q_w, k_w, v_w, ig_w, ig_b, fg_w, fg_b, on_w, skip_w, w_down)[0]

    def _L0_ffn_ref(x, router_w, w_gate, w_up, w_down):
        import jax, jax.numpy as jnp
        import numpy as np
        TOP_K = 2
        B, S, D = x.shape
        E = router_w.shape[0]
        xt = x.reshape(-1, D)
        logits = xt @ router_w.T
        topk_vals, topk_idx = jax.lax.top_k(logits, TOP_K)
        g = jax.nn.sigmoid(topk_vals)
        g = g / (g.sum(axis=-1, keepdims=True) + 1e-10)
        out = jnp.zeros_like(xt)
        for e in range(E):
            ge = jnp.sum(jnp.where(topk_idx == e, g, jnp.zeros_like(g)), axis=-1)
            h = jax.nn.silu(xt @ w_gate[e]) * (xt @ w_up[e])
            out = out + ge[:, None] * (h @ w_down[e])
        return out.reshape(B, S, D)
    x = L0_attn_hidden_states
    x = x + _L0_attn_ref(_layernorm(x, axis=-1), L0_attn_gate_w, L0_attn_ln_w, L0_attn_w_up, L0_attn_conv_w, L0_attn_conv_b, L0_attn_q_w, L0_attn_k_w, L0_attn_v_w, L0_attn_ig_w, L0_attn_ig_b, L0_attn_fg_w, L0_attn_fg_b, L0_attn_on_w, L0_attn_skip_w, L0_attn_w_down)
    x = x + _L0_ffn_ref(_layernorm(x, axis=-1), L0_ffn_router_w, L0_ffn_w_gate, L0_ffn_w_up, L0_ffn_w_down)
    return x

_drawn_inputs = setup_inputs


def setup_inputs(seed=0):
    import zlib

    import numpy as np

    out = dict(_drawn_inputs(seed))
    spreads = {'L0_attn_ln_w': (1.0, 0.6),
     'L0_attn_conv_b': (0.0, 0.8),
     'L0_attn_ig_b': (0.0, 2.0),
     'L0_attn_fg_b': (0.0, 0.1),
     'L0_attn_on_w': (1.0, 0.6),
     'L0_attn_skip_w': (1.0, 0.6)}
    factors = {'L0_attn_gate_w': 8.0,
     'L0_attn_w_up': 8.0,
     'L0_attn_conv_w': 8.0,
     'L0_attn_q_w': 8.0,
     'L0_attn_k_w': 8.0,
     'L0_attn_v_w': 8.0,
     'L0_attn_ig_w': 8.0,
     'L0_attn_w_down': 8.0}
    for name, (base, spread) in spreads.items():
        noise = np.random.default_rng([zlib.crc32(name.encode()), seed]).standard_normal(out[name].shape)
        drawn = base * np.exp(spread * noise) if base else spread * noise
        out[name] = jnp.asarray(drawn.astype(out[name].dtype))
    for name, factor in factors.items():
        out[name] = (out[name] * factor).astype(out[name].dtype)
    return out
```

```python
from contextlib import ExitStack

import concourse.bass as bass
from concourse import mybir

ALU = mybir.AluOpType
ACT = mybir.ActivationFunctionType
F32 = mybir.dt.float32
BF16 = mybir.dt.bfloat16
I32 = mybir.dt.int32
U32 = mybir.dt.uint32
AXX = mybir.AxisListType.X

P = 128
NTOK, D = 2048, 128
TT = NTOK // P
E, TOPK = 8, 2
I = 256
CH = I // P
NH, QB = 4, 4
DH = I // NH
NB = P // QB
TS = 256
HV = TS // P
NT = (TOPK * NTOK + E * (TS - 1)) // TS
NA = NT * HV
NP = NT // 2
PAIRS = TOPK * NTOK
EPS = 1e-5
CELL_EPS = 1e-6
EXP_MAX = 85.0
assert NT % 2 == 1 and NA <= P and P * 2 * TT == PAIRS

WC, WZ, KQ, WV = 0, I, 2 * I, 3 * I
GX, GC = 4 * I, 4 * I + NH
CB, ON, SK = GC + CH * NH, GC + CH * NH + CH, GC + CH * NH + 2 * CH
IB = SK + CH
REC = IB + NH


def at_least(eng, sem, value):
    if not isinstance(value, int) or value > 0:
        eng.wait_ge(sem, value)


def program(nc, hidden, gate_w, ln_w, w_up, conv_w, conv_b, q_w, k_w, v_w, ig_w, ig_b, on_w,
            skip_w, w_down, router_w, f_gate, f_up, f_down, out):
    with ExitStack() as ctx:
        def sb(name, shape, dt=F32):
            return ctx.enter_context(nc.sbuf_tensor(name, shape, dt))

        def sem(name):
            return ctx.enter_context(nc.semaphore(name))

        bank = [ctx.enter_context(nc.psum_tensor(f"bank{i}", [P, 512], F32)) for i in range(8)]

        xrows = [nc.dram_tensor(f"xrows{l}", [NTOK, D], F32, kind="Internal").ap() for l in range(2)]
        yrows = [nc.dram_tensor(f"yrows{l}", [PAIRS + NT * TS, D], F32, kind="Internal").ap() for l in range(2)]

        ident = sb("ident", [P, P])
        lower = sb("lower", [P, P], BF16)
        ones = sb("ones", [P, P], BF16)
        iota_p = sb("iota_p", [P, P], BF16)
        iota_a = sb("iota_a", [P, NA])
        part = sb("part", [P, 1])
        pairno = sb("pairno", [P, TT * TOPK])
        spare = sb("spare", [P, NA])
        ekey = sb("ekey", [P, E])
        tilecut = sb("tilecut", [P, E])
        upto = sb("upto", [P, E, E])
        tileno = sb("tileno", [P, NT + 1])
        blockmask = sb("blockmask", [P, NB])
        headmask = sb("headmask", [P, 2])
        centre = sb("centre", [P, P])
        headsum = sb("headsum", [P, CH, NH])
        headvar = sb("headvar", [P, CH, NH])
        neghalf = sb("neghalf", [P, TT])

        x = sb("x", [P, TT, D])
        x1 = sb("x1", [P, TT, D])
        xn = sb("xn", [P, TT, D])
        xres = x
        x1T = sb("x1T", [P, TT, P])
        bn = sb("bn", [P, TT, 6])
        mv = sb("mv", [P, TT, 2])
        veps = sb("veps", [P, 2, TT])
        rstd = sb("rstd", [P, 2, TT])

        lg = sb("lg", [P, TT, E])
        key = sb("key", [P, TT, E])
        top = sb("top", [P, TT, TOPK])
        kmax = sb("kmax", [P, TT])
        pick = sb("pick", [P, TT, TOPK, E])
        picked = sb("picked", [P, TT + 1, E], BF16)
        cmp8 = sb("cmp8", [P, E, E])
        ntile = sb("ntile", [P, E])
        cum = sb("cum", [P, E])
        before = sb("before", [P, E])
        place = sb("place", [P, TT, E])
        pslot = sb("pslot", [P, TT, TOPK, E])
        slot = sb("slot", [P, TT * TOPK])
        sloti = sb("sloti", [P, TT * TOPK], I32)
        loi = sb("loi", [P, TT * TOPK], I32)
        hii = sb("hii", [P, TT * TOPK], I32)
        lof = sb("lof", [P, TT * TOPK])
        hif = sb("hif", [P, TT * TOPK])
        cmpj = sb("cmpj", [1, NT + 1, E])
        ej = sb("ej", [1, NT + 1])
        expert = [sb(f"expert{l}", [1, NT + 1], I32) for l in range(2)]
        onehot = sb("onehot", [P, TT * TOPK, P], BF16)
        rhs = sb("rhs", [P, TT * TOPK, 3 * NA], BF16)
        perm = sb("perm", [P, 3 * NA])
        pairf = sb("pairf", [P, NA])
        unused = sb("unused", [P, NA])
        pairi = sb("pairi", [P, NA], U32)
        gidx = [sb(f"gidx{l}", [P, NA], U32) for l in range(2)]
        sidx = [sb(f"sidx{l}", [P, NA], U32) for l in range(2)]
        ex = sb("ex", [P, TT, TOPK])
        den = sb("den", [P, TT, TOPK])
        wt = sb("wt", [P, TT, TOPK])
        wsum = sb("wsum", [P, TT])
        wh = [sb(f"wh{l}", [P, TT, TOPK]) for l in range(2)]

        raw1 = sb("raw1", [64, 4 * P])
        raw2 = sb("raw2", [48, 4 * P])
        raw3 = sb("raw3", [64, P])
        gate = sb("gate", [P, E])
        qkvT = sb("qkvT", [P, QB, 64])
        igT = sb("igT", [P, NH, 48])
        parT = sb("parT", [P, 64])
        wraw = sb("wraw", [P, E, 2 * I])
        wl = sb("wl", [P, 2, I])
        blocks = sb("blocks", [P, 3 * E * CH, NB, QB])
        mT = sb("mT", [P, CH, P])
        mTs = sb("mTs", [P, CH, P])
        vT = sb("vT", [P, CH, P + NH])
        rec = sb("rec", [P, E, REC])
        wd1 = sb("wd1", [P, E, CH, D])
        gu = sb("gu", [P, E, 2, I])
        wd2 = sb("wd2", [P, E, CH, D])
        ypair = blocks[:, 0:2 * E * CH].rearrange("p m n b -> p m (n b)")

        gi = sb("gi", [P, 2, HV], U32)
        si = sb("si", [P, 2, HV], U32)
        rbuf = sb("rbuf", [P, 2, REC])
        gubuf = sb("gubuf", [P, 2, 2, I])
        xg = sb("xg", [P, 2, HV, D])
        xT = sb("xT", [P, 2, TS])
        pre = sb("pre", [P, 2, CH, TS])
        def tiles(buf, n):
            return buf[:].rearrange("p a b -> p (a b)")[:, n * 2 * I * 2:(n + 1) * 2 * I * 2]\
                .rearrange("p (b c t) -> p b c t", b=2, c=CH)

        thc, thz = tiles(xn, 0), tiles(xn, 1)
        sq, hs = tiles(x1T, 0), tiles(x1T, 1)
        ca, zz, von, prod = (tiles(wraw, n) for n in range(4))
        t1 = sb("t1", [P, CH, TS])
        h1 = sb("h1", [P, CH, TS])
        sbc = sb("sbc", [P, HV * NH, DH])
        yb = sb("yb", [P, 2, HV, D])
        nig0 = sb("nig0", [P, HV, NH])
        nig = sb("nig", [P, HV, NH])
        eig = sb("eig", [P, HV, NH])
        qks = sb("qks", [P, HV, NH])
        absqk = sb("absqk", [P, HV, NH])
        nrm = sb("nrm", [P, HV, NH])
        nrm6 = sb("nrm6", [P, HV, NH])
        rn = sb("rn", [P, HV, NH])
        cc = sb("cc", [P, HV, NH])
        c2 = sb("c2", [P, HV, NH])
        c2v = sb("c2v", [P, HV, NH])
        c2ve = sb("c2ve", [P, HV, NH])
        rh = sb("rh", [P, HV, NH])
        ss = sb("ss", [P, HV * NH])

        s_x, s_raw, s_gate, s_wraw, s_ib, s_late = (sem(n) for n in (
            "x_loaded", "raw_loaded", "gate_loaded", "wup_loaded", "igb_loaded", "late_loaded"))
        s_pool = sem("pool_step")
        s_const = sem("consts_ready")
        s_dve = sem("dve_step")
        s_veps = [sem(f"veps_ready{l}") for l in range(2)]
        s_rstd = [sem(f"rstd_ready{l}") for l in range(2)]
        s_x1 = [sem(f"normed_ready{l}") for l in range(2)]
        s_xn = sem("xn_ready")
        s_x1T = [sem(f"normedT_psum{l}") for l in range(2)]
        s_x1Tc = [sem(f"normedT_copied{l}") for l in range(2)]
        s_lg = [sem(f"logits_ready{l}") for l in range(2)]
        s_top = [sem(f"top_ready{l}") for l in range(2)]
        s_ex = [sem(f"topexp_ready{l}") for l in range(2)]
        s_picked = [sem(f"picked_ready{l}") for l in range(2)]
        s_rank = [sem(f"rank_ready{l}") for l in range(2)]
        s_hot = [sem(f"onehots_ready{l}") for l in range(2)]
        s_perm = [sem(f"perm_ready{l}") for l in range(2)]
        s_idx = [sem(f"indices_ready{l}") for l in range(2)]
        s_exp = [sem(f"experts_ready{l}") for l in range(2)]
        s_rows = [sem(f"xrows_stored{l}") for l in range(2)]
        s_parp, s_parT, s_blk, s_wl = sem("par_psum"), sem("par_copied"), sem("blocks_ready"), sem("wl_ready")
        s_pT, s_pV, s_pKQ, s_pWc, s_pWv = (sem(n) for n in ("mT_psum", "vT_psum", "kq_psum", "wc_psum", "wv_psum"))
        s_mT, s_vT, s_kq, s_wc, s_rec = (sem(n) for n in ("mT_copied", "vT_copied", "kq_copied", "wc_copied", "record_ready"))
        s_par2 = sem("params_in_record")
        s_gath = [[sem(f"gathered{l}{b}") for b in range(2)] for l in range(2)]
        s_scat = [[sem(f"scattered{l}{b}") for b in range(2)] for l in range(2)]
        s_wbuf = [[sem(f"weights_in{l}{b}") for b in range(2)] for l in range(2)]
        s_gi = [sem(f"gi_copied{l}") for l in range(2)]
        s_issue = sem("pool_issues")
        s_si = [sem(f"si_copied{l}") for l in range(2)]
        s_xtp = [sem(f"xT_psum{l}") for l in range(2)]
        s_xts = [sem(f"xT_copied{l}") for l in range(2)]
        s_y = [sem(f"y_psum{l}") for l in range(2)]
        s_yb = [sem(f"y_copied{l}") for l in range(2)]
        s_pc, s_vc, s_z, s_a, s_st, s_sbT = (sem(n) for n in (
            "conv_psum", "v_psum", "z_psum", "kqca_psum", "stats_psum", "scaleT_psum"))
        s_pre, s_thc, s_sq, s_von, s_thz, s_eig, s_sbc = (sem(n) for n in (
            "pre_ready", "tanh_conv", "sq_ready", "von_ready", "tanh_z", "exp_ig", "scale_spread"))
        s_nig, s_cell, s_stf, s_c2ve, s_rh, s_ss = (sem(n) for n in (
            "nig_ready", "cell_step", "stats_read", "var_ready", "rstd_h", "scale_ready"))
        s_ca, s_prod, s_zz, s_t1, s_h1, s_hs = (sem(n) for n in (
            "ca_ready", "prod_ready", "zz_ready", "t1_ready", "h1_ready", "hs_ready"))
        s_g, s_u, s_thg, s_gg, s_hh = (sem(n) for n in (
            "gate_psum", "up_psum", "tanh_gate", "gated", "ffn_h"))
        s_yin = [[sem(f"ypair_loaded{l}{c}") for c in range(4)] for l in range(2)]
        s_out = sem("out_ready")
        s_st_out = sem("out_stored")

        out_v = out.rearrange("b s d -> (b s) d").rearrange("(p i) d -> p i d", i=TT)
        x_v = hidden.rearrange("b s d -> (b s) d").rearrange("(p i) d -> p i d", i=TT)
        Lp, Rp, Mp = bank[7][:, 0:TT * E], bank[7][:, 128:128 + (TT + 1) * E], bank[7][:, 288:288 + 3 * NA][:, 0:138]
        Mp = bank[5][:, 0:3 * NA]
        XT, PC, VC, Z, A, ST, SB, Y = (bank[i] for i in range(8))
        qk = ST[:, 0:HV * 12].rearrange("p (h k) -> p h k", h=HV)[:, :, 0:4]
        var = ST[:, 0:HV * 12].rearrange("p (h k) -> p h k", h=HV)[:, :, 4:8]
        ig = ST[:, 0:HV * 12].rearrange("p (h k) -> p h k", h=HV)[:, :, 8:12]

        last0, last1 = (NT + 1) // 2, NT // 2
        block = ctx.enter_context(nc.Block())

        def steps(eng, step, lag):
            for b in range(2):
                step(0, b)
            with eng.Fori(1, NP) as u:
                for b in range(2):
                    step(u, b)
            for j in range(2 * NP, NT + lag):
                step(j // 2, j % 2)

        def active(u, b, back=0):
            return not isinstance(u, int) or 0 <= 2 * u + b - back < NT

        def earlier(u, b, back):
            return (u - (back - b + 1) // 2, (b - back) % 2)

        @block.sync
        def _(sp):
            h = TT // 2
            sp.dma_start(x[:, 0:h, :], x_v[:, 0:h, :]).then_inc(s_x, 16)
            sp.dma_start(x[:, h:TT, :], x_v[:, h:TT, :]).then_inc(s_x, 16)
            sp.dma_start(gate[:], gate_w).then_inc(s_gate, 16)
            sp.dma_start(wraw[:], w_up.rearrange("e d n -> d e n")).then_inc(s_wraw, 16)
            sp.dma_start(wd1[:], w_down.rearrange("e (c p) d -> p e c d", p=P)).then_inc(s_late, 16)
            sp.dma_start(gu[:, :, 0, :], f_gate.rearrange("e d n -> d e n")).then_inc(s_late, 16)
            sp.dma_start(gu[:, :, 1, :], f_up.rearrange("e d n -> d e n")).then_inc(s_late, 16)
            sp.dma_start(wd2[:], f_down.rearrange("e (c p) d -> p e c d", p=P)).then_inc(s_late, 16)

            sp.wait_ge(s_xn, 1)
            sp.dma_start(xrows[0].rearrange("(p i) d -> p i d", i=TT), xn[:]).then_inc(s_rows[0], 16)

            sp.wait_ge(s_exp[0], 1)
            sp.wait_ge(s_rec, E)
            sp.wait_ge(s_par2, 4)
            sp.wait_ge(s_kq, 2 * E)
            sp.wait_ge(s_wc, E)

            def load1(u, b):
                if not active(u, b):
                    return
                j = 2 * u + b
                e = sp.value_load(expert[0][0:1, bass.ds(j, 1)], min_val=0, max_val=E - 1)
                at_least(sp, s_st, j - 1)
                at_least(sp, s_von, j - 1)
                at_least(sp, s_h1, j - 1)
                sp.dma_start(rbuf[:, b, :], rec[:, bass.ds(e, 1), :].rearrange("p a n -> p (a n)"))\
                    .then_inc(s_wbuf[0][b], 16)
            steps(sp, load1, 0)

            def load_pairs(l):
                sp.wait_ge(s_scat[l][0], 32 * last0)
                sp.wait_ge(s_scat[l][1], 32 * last1)
                yv = yrows[l][0:PAIRS, :].rearrange("(p m) d -> p m d", p=P)
                for c in range(4):
                    m = PAIRS // P // 4
                    sp.dma_start(ypair[:, c * m:(c + 1) * m, :], yv[:, c * m:(c + 1) * m, :])\
                        .then_inc(s_yin[l][c], 16)
            load_pairs(0)

            sp.wait_ge(s_x1[1], 1)
            sp.dma_start(xrows[1].rearrange("(p i) d -> p i d", i=TT), x1[:]).then_inc(s_rows[1], 16)
            sp.wait_ge(s_exp[1], 1)
            sp.wait_ge(s_late, 64)

            def load2(u, b):
                if not active(u, b):
                    return
                j = 2 * u + b
                e = sp.value_load(expert[1][0:1, bass.ds(j, 1)], min_val=0, max_val=E - 1)
                at_least(sp, s_u, j - 1)
                sp.dma_start(gubuf[:, b, :, :], gu[:, bass.ds(e, 1), :, :].rearrange("p a g n -> p (a g) n"))\
                    .then_inc(s_wbuf[1][b], 16)
            steps(sp, load2, 0)
            load_pairs(1)
            for c in range(4):
                m = TT // 4
                sp.wait_ge(s_out, c + 1)
                sp.dma_start(out_v[:, c * m:(c + 1) * m, :], xres[:, c * m:(c + 1) * m, :])\
                    .then_inc(s_st_out, 16)
            sp.wait_ge(s_st_out, 64)

        @block.gpsimd
        def _(pool):
            g = nc.gpsimd
            count = [0]

            def done(ins):
                count[0] += 1
                ins.then_inc(s_pool, 1)
                pool.wait_ge(s_pool, count[0])

            def select(t, pattern, base, cm, op=ALU.is_ge):
                done(g.affine_select(out=t, in_=t, compare_op=op, fill=0.0, base=base,
                                     pattern=pattern, channel_multiplier=cm))

            done(g.memset(ident[:], 0.0))
            done(g.affine_select(out=ident[:], in_=ident[:], compare_op=ALU.not_equal, fill=1.0, base=0,
                                 pattern=[[-1, P]], channel_multiplier=1))
            g.memset(picked[:], 0.0)
            g.memset(neghalf[:], -0.5)
            done(g.memset(blockmask[:], 1.0))
            select(blockmask[:], [[-QB, NB]], 0, 1)
            select(blockmask[:], [[QB, NB]], QB - 1, -1)
            done(g.memset(headmask[:], 1.0))
            select(headmask[:], [[-DH, 2]], 0, 1)
            select(headmask[:], [[DH, 2]], DH - 1, -1)
            g.memset(headsum[:], 0.0)
            done(g.memset(headvar[:], 0.0))
            for c in range(CH):
                g.tensor_scalar(headsum[:, c, 2 * c:2 * c + 2], headmask[:], DH ** -0.5 / 4, None, ALU.mult)
                g.tensor_scalar(headvar[:, c, 2 * c:2 * c + 2], headmask[:], 1.0 / DH, None, ALU.mult)
            done(g.tensor_scalar(centre[:].rearrange("p (k r) -> p k r", k=2),
                                 headmask[:].unsqueeze(2).to_broadcast([P, 2, DH]), -1.0 / DH, None, ALU.mult))
            done(g.tensor_tensor(centre[:], centre[:], ident[:], ALU.add))
            small = dict(allow_small_or_imprecise_dtypes=True)
            done(g.iota(ekey[:], pattern=[[-1, E]], base=E, channel_multiplier=0, **small))
            done(g.memset(lower[:], 1.0))
            select(lower[:], [[1, P]], -1, -1)
            g.memset(ones[:], 1.0)
            done(g.memset(upto[:], 1.0))
            select(upto[:], [[1, E], [-1, E]], 0, 0)
            g.iota(tilecut[:], pattern=[[TS, E]], base=0, channel_multiplier=0, **small)
            g.iota(tileno[:], pattern=[[1, NT + 1]], base=0, channel_multiplier=0, **small)
            g.iota(iota_p[:], pattern=[[1, P]], base=0, channel_multiplier=0, **small)
            g.iota(iota_a[:], pattern=[[1, NA]], base=0, channel_multiplier=0, **small)
            g.iota(part[:], pattern=[[0, 1]], base=0, channel_multiplier=1, **small)
            g.iota(pairno[:], pattern=[[1, TT * TOPK]], base=0, channel_multiplier=0, **small)
            done(g.iota(spare[:], pattern=[[P, NA]], base=PAIRS, channel_multiplier=1, **small))
            g.memset(cmpj[:], 0.0).then_inc(s_const, 1)

            for k in range(2):
                pool.wait_ge(s_veps[0], k + 1)
                g.tensor_tensor(rstd[:, k, :], veps[:, k, :], neghalf[:], ALU.pow).then_inc(s_rstd[0], 1)

            pool.wait_ge(s_parT, 1)
            n = E * CH
            for m in range(3):
                g.tensor_tensor(
                    blocks[:, m * n:(m + 1) * n],
                    blockmask[:][:, None, :, None].to_broadcast([P, n, NB, QB]),
                    qkvT[:, :, m * n:(m + 1) * n].rearrange("p b m -> p m b").unsqueeze(2).to_broadcast([P, n, NB, QB]),
                    ALU.mult).then_inc(s_blk, 1)

            def gather(l, u, b, used):
                if not active(u, b):
                    return
                j = 2 * u + b
                col = pool.snap(HV * j)
                at_least(pool, used, j - 1)
                g.tensor_copy(gi[:, b, :], gidx[l][:, bass.ds(col, HV)]).then_inc(s_gi[l], 1)
                pool.wait_ge(s_rows[l], 16)
                pool.wait_ge(s_gi[l], j + 1)
                pool.sem_inc(s_issue, 1)
                for h in range(HV):
                    g.indirect_dma_start(
                        xg[:, b, h, :], None, xrows[l], bass.IndirectOffsetOnAxis(ap=gi[:, b, h:h + 1], axis=0)).then_inc(s_gath[l][b], 16)

            def scatter(l, u, b):
                if not active(u, b):
                    return
                j = 2 * u + b
                col = pool.snap(HV * j)
                at_least(pool, s_scat[l][b], 32 * u)
                g.tensor_copy(si[:, b, :], sidx[l][:, bass.ds(col, HV)]).then_inc(s_si[l], 1)
                pool.wait_ge(s_si[l], j + 1)
                pool.wait_ge(s_yb[l], j + 1)
                pool.sem_inc(s_issue, 1)
                for h in range(HV):
                    g.indirect_dma_start(
                        yrows[l], bass.IndirectOffsetOnAxis(ap=si[:, b, h:h + 1], axis=0), yb[:, b, h, :], None).then_inc(s_scat[l][b], 16)

            pool.wait_ge(s_idx[0], 1)
            gather(0, 0, 0, s_xtp[0])

            def step1(u, b):
                gather(0, *earlier(u, b, -1), s_xtp[0])
                k, kb = earlier(u, b, 1)
                if active(k, kb):
                    pool.wait_ge(s_c2ve, 2 * k + kb + 1)
                    at_least(pool, s_ss, 2 * k + kb)
                    g.tensor_tensor(rh[:], c2ve[:], neghalf[:, 0:8].rearrange("p (h k) -> p h k", h=HV),
                                    ALU.pow).then_inc(s_rh, 1)
                scatter(0, *earlier(u, b, 2))
            steps(pool, step1, 2)

            pool.wait_ge(s_veps[1], 1)
            g.tensor_tensor(rstd[:, 0, :], veps[:, 0, :], neghalf[:], ALU.pow).then_inc(s_rstd[1], 1)
            pool.wait_ge(s_idx[1], 1)
            gather(1, 0, 0, s_xtp[1])

            def step2(u, b):
                gather(1, *earlier(u, b, -1), s_xtp[1])
                scatter(1, *earlier(u, b, 1))
            steps(pool, step2, 1)

        @block.scalar
        def _(act):
            a = nc.scalar
            r = E * CH
            for m, w in enumerate((q_w, k_w, v_w)):
                act.dma_start(raw1[m * r:(m + 1) * r, :], w.rearrange("e (c n) o b -> (e c) (n o b)", c=CH)).then_inc(s_raw, 16)
            act.dma_start(raw1[3 * r:4 * r, :], conv_w.rearrange("e (c p) k -> (e c) (p k)", c=CH)).then_inc(s_raw, 16)
            act.dma_start(raw2[:], ig_w.rearrange("e (s p) h -> (e s) (p h)", p=P)).then_inc(s_raw, 16)
            for m, w in enumerate((conv_b, on_w, skip_w)):
                act.dma_start(raw3[m * r:(m + 1) * r, :], w.rearrange("e (c p) -> (e c) p", c=CH)).then_inc(s_raw, 16)
            act.dma_start(raw3[3 * r:3 * r + E, :], ln_w).then_inc(s_raw, 16)
            act.dma_start(raw3[3 * r + E:3 * r + 2 * E, :], router_w).then_inc(s_raw, 16)
            act.dma_start(rec[:, :, IB:IB + NH], ig_b.unsqueeze(0).to_broadcast([P, E, NH])).then_inc(s_ib, 16)

            act.wait_ge(s_parp, 1)
            a.activation(qkvT[:].rearrange("p b m -> p (b m)"), bank[0][:, 0:4 * 64], ACT.Copy)
            a.activation(igT[:].rearrange("p h m -> p (h m)"), bank[1][:, 0:4 * 48], ACT.Copy)
            a.activation(parT[:], bank[2][:, 0:64], ACT.Copy).then_inc(s_parT, 1)
            act.wait_ge(s_parT, 1)
            act.wait_ge(s_ib, 16)
            for m, (col, scale) in enumerate(((CB, 1.0), (ON, 1.0), (SK, 0.5))):
                a.activation(rec[:, :, col:col + CH], parT[:, m * r:(m + 1) * r].rearrange("p (e c) -> p e c", c=CH),
                             ACT.Copy, scale=scale).then_inc(s_par2, 1)
            act.wait_ge(s_wraw, 16)

            def transposed(l):
                for q in range(4):
                    act.wait_ge(s_x1T[l], q + 1)
                    a.activation(x1T[:, 4 * q:4 * q + 4, :].rearrange("p i t -> p (i t)"), bank[5 + q % 2][:, :],
                                 ACT.Copy).then_inc(s_x1Tc[l], 1)

            def fold(e):
                at = 3 * r + e
                if e >= 2:
                    act.wait_ge(s_pT, e - 1)
                a.activation(wl[:, e % 2, :], wraw[:, e, 0:I], ACT.Copy, scale=parT[:, at:at + 1]).then_inc(s_wl, 1)
                a.activation(rec[:, e, WZ:WZ + I], wraw[:, e, I:2 * I], ACT.Copy, scale=parT[:, at:at + 1])

            def prepare(e):
                if e + 1 < E:
                    fold(e + 1)
                act.wait_ge(s_pT, e + 1)
                if e:
                    act.wait_ge(s_pWv, e)
                a.activation(mT[:].rearrange("p c t -> p (c t)"), bank[0][:, 0:I], ACT.Copy)
                for c in range(CH):
                    at = 3 * r + e * CH + c
                    a.activation(mTs[:, c, :], bank[0][:, c * P:(c + 1) * P], ACT.Copy,
                                 scale=qkvT[:, 3, at:at + 1]).then_inc(s_mT, 1)
                act.wait_ge(s_pV, e + 1)
                a.activation(vT[:].rearrange("p c t -> p (c t)"), bank[1][:, 0:CH * (P + NH)], ACT.Copy).then_inc(s_vT, 1)
                act.wait_ge(s_pKQ, e + 1)
                a.activation(rec[:, e, KQ:KQ + I], bank[2][:, 0:I], ACT.Copy).then_inc(s_kq, 1)
                a.activation(rec[:, e, GC:GC + CH * NH], bank[2][:, I:I + CH * NH], ACT.Copy, scale=0.5).then_inc(s_kq, 1)
                act.wait_ge(s_pWc, e + 1)
                a.activation(rec[:, e, WC:WC + I], bank[3][:, 0:I], ACT.Copy).then_inc(s_wc, 1)
                act.wait_ge(s_pWv, e + 1)
                a.activation(rec[:, e, WV:WV + I + NH], bank[4][:, 0:I + NH], ACT.Copy).then_inc(s_rec, 1)

            fold(0)
            transposed(0)
            for e in range(2):
                prepare(e)
            act.wait_ge(s_top[0], 1)
            a.activation(ex[:, :, 0], den[:, :, 0], ACT.Exp).then_inc(s_ex[0], 1)
            for e in range(2, E):
                prepare(e)
            act.wait_ge(s_par2, 3)
            act.wait_ge(s_rec, E)
            a.activation(neghalf[:, 0:1], neghalf[:, 0:1], ACT.Copy).then_inc(s_par2, 1)

            def step1(u, b):
                j = 2 * u + b
                up, k1, k2 = active(u, b), active(u, b, 1), active(u, b, 2)
                if up:
                    act.wait_ge(s_xtp[0], j + 1)
                    a.activation(xT[:, b, :], XT[:, 0:TS], ACT.Copy).then_inc(s_xts[0], 1)
                if k1:
                    act.wait_ge(s_nig, j)
                    a.activation(eig[:], nig[:], ACT.Exp).then_inc(s_eig, 1)
                if up:
                    act.wait_ge(s_pc, j + 1)
                    act.wait_ge(s_wbuf[0][b], 16 * (u + 1))
                    at_least(act, s_ca, j - 1)
                    for c in range(CH):
                        a.activation(pre[:, b, c, :], PC[:, c * TS:(c + 1) * TS], ACT.Identity,
                                     bias=rbuf[:, b, CB + c:CB + c + 1]).then_inc(s_pre, 1)
                    act.wait_ge(s_pre, 2 * j + 2)
                    a.activation(thc[:, b], pre[:, b], ACT.Tanh, scale=0.5).then_inc(s_thc, 1)
                    act.wait_ge(s_vc, j + 1)
                    a.activation(sq[:, b], VC[:].rearrange("p (c t) -> p c t", c=CH), ACT.Square).then_inc(s_sq, 1)
                    at_least(act, s_t1, j - 1)
                    for c in range(CH):
                        ins = a.activation(von[:, b, c, :], VC[:, c * TS:(c + 1) * TS], ACT.Copy,
                                           scale=rbuf[:, b, ON + c:ON + c + 1])
                    ins.then_inc(s_von, 1)
                if k1:
                    act.wait_ge(s_ss, j)
                    at_least(act, s_sbT, j - 1)
                    a.activation(sbc[:], ss[:].unsqueeze(2).to_broadcast([P, HV * NH, DH]), ACT.Copy).then_inc(s_sbc, 1)
                if up:
                    act.wait_ge(s_z, j + 1)
                    at_least(act, s_zz, j - 1)
                    a.activation(thz[:, b], Z[:].rearrange("p (c t) -> p c t", c=CH), ACT.Tanh, scale=0.5).then_inc(s_thz, 1)
                if k2:
                    y_out(0, *earlier(u, b, 2), Y)

            def y_out(l, k, kb, src):
                act.wait_ge(s_y[l], 2 * k + kb + 1)
                at_least(act, s_scat[l][kb], 32 * k)
                a.activation(yb[:, kb], src[:, 0:TS].rearrange("p (h d) -> p h d", h=HV), ACT.Copy).then_inc(s_yb[l], 1)
            steps(act, step1, 2)

            transposed(1)
            act.wait_ge(s_top[1], 1)
            a.activation(ex[:], den[:], ACT.Exp, scale=-1.0).then_inc(s_ex[1], 1)

            def step2(u, b):
                j = 2 * u + b
                if active(u, b):
                    act.wait_ge(s_xtp[1], j + 1)
                    a.activation(xT[:, b, :], bank[b][:, 0:TS], ACT.Copy).then_inc(s_xts[1], 1)
                    act.wait_ge(s_g, j + 1)
                    at_least(act, s_gg, j - 1)
                    a.activation(thc[:, b], bank[2 + b][:].rearrange("p (c t) -> p c t", c=CH), ACT.Tanh, scale=0.5).then_inc(s_thg, 1)
                if active(u, b, 1):
                    k, kb = earlier(u, b, 1)
                    y_out(1, k, kb, bank[6 + kb])
            steps(act, step2, 1)

        @block.tensor
        def _(pe):
            t = nc.tensor
            r = E * CH
            pe.wait_ge(s_pool, 2)
            pe.wait_ge(s_raw, 16 * 10)
            for b in range(QB):
                t.transpose(bank[0][:, b * 64:(b + 1) * 64], raw1[:, b:4 * P:4], ident[0:64, 0:64])
            for h in range(NH):
                t.transpose(bank[1][:, h * 48:(h + 1) * 48], raw2[:, h:4 * P:4], ident[0:48, 0:48])
            t.transpose(bank[2][:, 0:64], raw3[:], ident[0:64, 0:64]).then_inc(s_parp, 1)

            def route_transposes(l):
                for q in range(4):
                    if l == 0:
                        pe.wait_ge(s_x1[0], 4 * q + 4)
                    else:
                        pe.wait_ge(s_x1[1], 1)
                    if q >= 2:
                        pe.wait_ge(s_x1Tc[l], q - 1)
                    for i in range(4):
                        ins = t.transpose(bank[5 + q % 2][:, i * P:(i + 1) * P], x1[:, 4 * q + i, :], ident[:])
                    ins.then_inc(s_x1T[l], 1)

            def route_logits(l, w):
                pe.wait_ge(s_x1Tc[l], 4)
                for i in range(TT):
                    ins = t.matmul(Lp[:, i * E:(i + 1) * E], x1T[:, i, :], w, start=True, stop=True)
                ins.then_inc(s_lg[l], 1)

            def route_rank(l):
                pe.wait_ge(s_picked[l], 1)
                pe.wait_ge(s_const, 1)
                pk = picked[:].rearrange("p i e -> p (i e)")
                t.matmul(Rp, lower[:], pk, start=True, stop=False, skip_group_check=True)
                for i in range(TT):
                    n = TT - i
                    ins = t.matmul(Rp[:, (i + 1) * E:].rearrange("p (n e) -> p n e", e=E), ones[:],
                                   picked[:, i:i + 1, :].to_broadcast([P, n, E]), start=False, stop=(i == TT - 1),
                                   skip_group_check=True)
                ins.then_inc(s_rank[l], 1)

            def route_perm(l):
                n = TT * TOPK
                for c in range(n):
                    if c % 8 == 0:
                        pe.wait_ge(s_hot[l], c // 8 + 1)
                    ins = t.matmul(Mp, onehot[:, c, :], rhs[:, c, :], start=(c == 0), stop=(c == n - 1))
                ins.then_inc(s_perm[l], 1)

            def prepare(e):
                pe.wait_ge(s_wl, e + 1)
                if e:
                    pe.wait_ge(s_mT, 2 * e)
                for c in range(CH):
                    ins = t.transpose(bank[0][:, c * P:(c + 1) * P], wl[:, e % 2, c * P:(c + 1) * P], ident[:])
                ins.then_inc(s_pT, 1)
                if e == 0:
                    pe.wait_ge(s_blk, 3)
                else:
                    pe.wait_ge(s_vT, e)
                for c in range(CH):
                    vb = blocks[:, 2 * r + e * CH + c].rearrange("p n b -> p (n b)")
                    o = c * (P + NH)
                    t.matmul(bank[1][:, o:o + P], vb, centre[:], start=True, stop=True)
                    ins = t.matmul(bank[1][:, o + P:o + P + NH], vb, igT[:, :, 6 * e + 4 + c], start=True, stop=True)
                ins.then_inc(s_pV, 1)
                if e:
                    pe.wait_ge(s_kq, 2 * e)
                for c in range(CH):
                    qb = blocks[:, e * CH + c].rearrange("p n b -> p (n b)")
                    kb = blocks[:, r + e * CH + c].rearrange("p n b -> p (n b)")
                    t.matmul(bank[2][:, c * P:(c + 1) * P], kb, qb, start=True, stop=True)
                    t.matmul(bank[2][:, I + c * NH:I + (c + 1) * NH], qb, igT[:, :, 6 * e + c], start=True, stop=False)
                    ins = t.matmul(bank[2][:, I + c * NH:I + (c + 1) * NH], kb, igT[:, :, 6 * e + 2 + c], start=False, stop=True)
                ins.then_inc(s_pKQ, 1)
                pe.wait_ge(s_mT, 2 * e + 2)
                if e:
                    pe.wait_ge(s_wc, e)
                for c in range(CH):
                    ins = t.transpose(bank[3][:, c * P:(c + 1) * P], mTs[:, c, :], ident[:])
                ins.then_inc(s_pWc, 1)
                pe.wait_ge(s_vT, e + 1)
                if e:
                    pe.wait_ge(s_rec, e)
                for c in range(CH):
                    t.matmul(bank[4][:, c * P:(c + 1) * P], mT[:, c, :], vT[:, c, 0:P], start=True, stop=True)
                for c in range(CH):
                    ins = t.matmul(bank[4][:, I:I + NH], mT[:, c, :], vT[:, c, P:P + NH], start=(c == 0), stop=(c == CH - 1))
                ins.then_inc(s_pWv, 1)

            route_transposes(0)
            pe.wait_ge(s_gate, 16)
            route_logits(0, gate[:])
            pe.wait_ge(s_parT, 1)
            for e in range(2):
                prepare(e)
            route_rank(0)
            for e in range(2, 4):
                prepare(e)
            route_perm(0)
            for e in range(4, E):
                prepare(e)
            pe.wait_ge(s_rec, E)
            pe.wait_ge(s_idx[0], 1)
            pe.wait_ge(s_late, 64)

            def in_transposes(l, u, b, dst):
                pe.wait_ge(s_gath[l][b], 32 * (u + 1))
                for h in range(HV):
                    ins = t.transpose(dst[:, h * P:(h + 1) * P], xg[:, b, h, :], ident[:])
                ins.then_inc(s_xtp[l], 1)

            def down(k, kb, src, wd, l, dst):
                e = pe.value_load(expert[l][0:1, bass.ds(2 * k + kb, 1)], min_val=0, max_val=E - 1)
                for h in range(HV):
                    for c in range(CH):
                        ins = t.matmul(dst[:, h * D:(h + 1) * D], src[:, kb, c, h * P:(h + 1) * P],
                                       wd[:, bass.ds(e, 1), c, :].rearrange("p a d -> p (a d)"),
                                       start=(c == 0), stop=(c == CH - 1))
                ins.then_inc(s_y[l], 1)

            def step1(u, b):
                j = 2 * u + b
                up, k1, k2 = active(u, b), active(u, b, 1), active(u, b, 2)

                def project(dst, col):
                    for c in range(CH):
                        ins = t.matmul(dst[:, c * TS:(c + 1) * TS], rbuf[:, b, col + c * P:col + (c + 1) * P], xT[:, b, :],
                                       start=True, stop=True)
                    return ins

                if up:
                    in_transposes(0, u, b, XT)
                    pe.wait_ge(s_xts[0], j + 1)
                    pe.wait_ge(s_wbuf[0][b], 16 * (u + 1))
                    at_least(pe, s_pre, 2 * j)
                    project(PC, WC).then_inc(s_pc, 1)
                if k2:
                    k, kb = earlier(u, b, 2)
                    pe.wait_ge(s_hs, 2 * k + kb + 1)
                    at_least(pe, s_yb[0], 2 * k + kb)
                    down(k, kb, hs, wd1, 0, Y)
                if up:
                    at_least(pe, s_von, j)
                    project(VC, WV).then_inc(s_vc, 1)
                    at_least(pe, s_zz, j)
                    project(Z, WZ).then_inc(s_z, 1)
                    pe.wait_ge(s_ca, j + 1)
                    at_least(pe, s_prod, j)
                    for c in range(CH):
                        ins = t.matmul(A[:, c * TS:(c + 1) * TS], rbuf[:, b, KQ + c * P:KQ + (c + 1) * P], ca[:, b, c, :],
                                       start=True, stop=True)
                    ins.then_inc(s_a, 1)
                    pe.wait_ge(s_sq, j + 1)
                    at_least(pe, s_stf, j)
                    for h in range(HV):
                        tok = slice(h * P, (h + 1) * P)
                        for c in range(CH):
                            t.matmul(var[:, h, :], sq[:, b, c, tok], headvar[:, c, :], start=(c == 0), stop=(c == CH - 1))
                        t.matmul(ig[:, h, :], xT[:, b, tok], rbuf[:, b, GX:GX + NH], start=True, stop=False)
                        for c in range(CH):
                            t.matmul(ig[:, h, :], ca[:, b, c, tok], rbuf[:, b, GC + c * NH:GC + (c + 1) * NH],
                                     start=False, stop=(c == CH - 1))
                if k1:
                    k, kb = earlier(u, b, 1)
                    pe.wait_ge(s_sbc, j)
                    at_least(pe, s_t1, j - 1)
                    for c in range(CH):
                        for h in range(HV):
                            o = c * TS + h * P
                            ins = t.transpose(SB[:, o:o + P],
                                              sbc[:, h * NH + 2 * c:h * NH + 2 * c + 2, :].rearrange("p k d -> p (k d)"), ident[:])
                    ins.then_inc(s_sbT, 1)
                if up:
                    pe.wait_ge(s_prod, j + 1)
                    for h in range(HV):
                        for c in range(CH):
                            ins = t.matmul(qk[:, h, :], prod[:, b, c, h * P:(h + 1) * P], headsum[:, c, :],
                                           start=(c == 0), stop=(c == CH - 1))
                    ins.then_inc(s_st, 1)
            steps(pe, step1, 2)

            route_transposes(1)
            route_logits(1, parT[:, 3 * r + E:3 * r + 2 * E])
            route_rank(1)
            route_perm(1)
            pe.wait_ge(s_idx[1], 1)

            def step2(u, b):
                j = 2 * u + b
                if active(u, b):
                    in_transposes(1, u, b, bank[b])
                    pe.wait_ge(s_xts[1], j + 1)
                    pe.wait_ge(s_wbuf[1][b], 16 * (u + 1))
                    at_least(pe, s_hh, j - 1)
                    for which, done in ((0, s_g), (1, s_u)):
                        for c in range(CH):
                            ins = t.matmul(bank[2 + 2 * which + b][:, c * TS:(c + 1) * TS],
                                           gubuf[:, b, which, c * P:(c + 1) * P], xT[:, b, :], start=True, stop=True)
                        ins.then_inc(done, 1)
                if active(u, b, 1):
                    k, kb = earlier(u, b, 1)
                    pe.wait_ge(s_hh, 2 * k + kb + 1)
                    at_least(pe, s_yb[1], 2 * k + kb - 1)
                    down(k, kb, hs, wd2, 1, bank[6 + kb])
            steps(pe, step2, 1)

        @block.vector
        def _(dve):
            v = nc.vector
            count = [0]

            def done(ins):
                count[0] += 1
                ins.then_inc(s_dve, 1)
                dve.wait_ge(s_dve, count[0])

            def wide(ap, shape):
                return ap.to_broadcast(shape)

            def stats(src, cols):
                for i in cols:
                    ins = v.bn_stats(bn[:, i, :], src[:, i, :])
                done(ins)
                for i in cols:
                    ins = v.bn_aggr(mv[:, i, :], bn[:, i, :])
                return ins

            def route(l):
                dve.wait_ge(s_lg[l], 1)
                done(v.tensor_copy(lg[:], Lp.rearrange("p (i e) -> p i e", e=E)))
                row = [P, TT, E]
                for k in range(TOPK):
                    done(v.tensor_reduce(top[:, :, k], lg[:], AXX, ALU.max))
                    done(v.tensor_tensor(key[:], lg[:], wide(top[:, :, k:k + 1], row), ALU.is_equal))
                    done(v.tensor_tensor(key[:], key[:], wide(ekey[:].unsqueeze(1), row), ALU.mult))
                    done(v.tensor_reduce(kmax[:], key[:], AXX, ALU.max))
                    done(v.tensor_tensor(pick[:, :, k, :], key[:], wide(kmax[:].unsqueeze(2), row), ALU.is_equal))
                    if k == 0:
                        done(v.scalar_tensor_tensor(lg[:], pick[:, :, 0, :], -1e30, lg[:], ALU.mult, ALU.add))
                v.tensor_tensor(picked[:, 0:TT, :], pick[:, :, 0, :], pick[:, :, 1, :], ALU.add).then_inc(s_picked[l], 1)
                if l == 0:
                    v.tensor_tensor(den[:, :, 0], top[:, :, 1], top[:, :, 0], ALU.subtract).then_inc(s_top[0], 1)
                else:
                    v.tensor_scalar(den[:], top[:], -EXP_MAX, None, ALU.max).then_inc(s_top[1], 1)
                dve.wait_ge(s_rank[l], 1)
                sq8 = [P, E, E]
                done(v.tensor_tensor(cmp8[:], wide(Rp[:, TT * E:].unsqueeze(2), sq8), wide(tilecut[:].unsqueeze(1), sq8), ALU.is_gt))
                done(v.tensor_reduce(ntile[:], cmp8[:], AXX, ALU.add))
                done(v.tensor_tensor(cmp8[:], wide(ntile[:].unsqueeze(1), sq8), upto[:], ALU.mult))
                done(v.tensor_reduce(cum[:], cmp8[:], AXX, ALU.add))
                jrow = [1, NT + 1, E]
                done(v.tensor_tensor(cmpj[:], wide(cum[0:1, :].unsqueeze(1), jrow), wide(tileno[0:1, :].unsqueeze(2), jrow), ALU.is_le))
                done(v.tensor_reduce(ej[:], cmpj[:], AXX, ALU.add))
                v.tensor_scalar(expert[l][:], ej[:], float(E - 1), None, ALU.min).then_inc(s_exp[l], 1)
                done(v.tensor_tensor(before[:], cum[:], ntile[:], ALU.subtract))
                done(v.scalar_tensor_tensor(place[:], wide(before[:].unsqueeze(1), row), float(TS),
                                            Rp[:, 0:TT * E].rearrange("p (i e) -> p i e", e=E), ALU.mult, ALU.add))
                done(v.tensor_tensor(pslot[:], pick[:], wide(place[:].unsqueeze(2), [P, TT, TOPK, E]), ALU.mult))
                done(v.tensor_reduce(slot[:].rearrange("p (i k) -> p i k", k=TOPK), pslot[:], AXX, ALU.add))
                done(v.tensor_copy(sloti[:], slot[:]))
                v.tensor_scalar(loi[:], sloti[:], P - 1, None, ALU.bitwise_and)
                done(v.tensor_scalar(hii[:], sloti[:], 7, None, ALU.logical_shift_right))
                v.tensor_copy(lof[:], loi[:])
                done(v.tensor_copy(hif[:], hii[:]))
                n = TT * TOPK
                used = rhs[:, :, 2 * NA:3 * NA]
                done(v.tensor_tensor(used, wide(hif[:].unsqueeze(2), [P, n, NA]), wide(iota_a[:].unsqueeze(1), [P, n, NA]), ALU.is_equal))
                v.tensor_scalar(rhs[:, :, 0:NA], used, part[:, 0:1], None, ALU.mult)
                v.tensor_tensor(rhs[:, :, NA:2 * NA], used, wide(pairno[:].unsqueeze(2), [P, n, NA]), ALU.mult)
                for c in range(n):
                    ins = v.tensor_scalar(onehot[:, c, :], iota_p[:], lof[:, c:c + 1], None, ALU.is_equal)
                    if c % 8 == 7:
                        ins.then_inc(s_hot[l], 1)
                dve.wait_ge(s_ex[l], 1)
                if l == 0:
                    done(v.tensor_scalar(den[:, :, 1], ex[:, :, 0], 1.0, None, ALU.add))
                    done(v.reciprocal(wt[:, :, 0], den[:, :, 1]))
                    done(v.tensor_tensor(wt[:, :, 1], ex[:, :, 0], wt[:, :, 0], ALU.mult))
                    v.tensor_tensor(wsum[:], wt[:, :, 0], wt[:, :, 1], ALU.add)
                    done(v.tensor_scalar(wh[0][:], wt[:], 0.5, None, ALU.mult))
                else:
                    done(v.tensor_scalar(den[:], ex[:], 1.0, None, ALU.add))
                    done(v.reciprocal(wt[:], den[:]))
                    done(v.tensor_tensor(wsum[:], wt[:, :, 0], wt[:, :, 1], ALU.add))
                    done(v.tensor_scalar(wsum[:], wsum[:], 1e-10, None, ALU.add))
                    done(v.reciprocal(kmax[:], wsum[:]))
                    done(v.scalar_tensor_tensor(wh[1][:], wt[:], 0.5, wide(kmax[:].unsqueeze(2), [P, TT, TOPK]), ALU.mult, ALU.mult))
                dve.wait_ge(s_perm[l], 1)
                done(v.tensor_copy(perm[:], Mp))
                done(v.scalar_tensor_tensor(pairf[:], perm[:, 0:NA], float(TOPK * TT), perm[:, NA:2 * NA], ALU.mult, ALU.add))
                v.tensor_tensor(unused[:], perm[:, 2 * NA:3 * NA], spare[:], ALU.mult)
                done(v.tensor_copy(pairi[:], pairf[:]))
                v.tensor_scalar(gidx[l][:], pairi[:], 1, None, ALU.logical_shift_right)
                done(v.tensor_tensor(unused[:], spare[:], unused[:], ALU.subtract))
                v.tensor_tensor(sidx[l][:], pairf[:], unused[:], ALU.add).then_inc(s_idx[l], 1)

            dve.wait_ge(s_x, 32)
            done(stats(x, range(TT)))
            done(v.tensor_scalar(veps[:, 0, :], mv[:, :, 1], EPS, None, ALU.add))
            v.tensor_copy(kmax[:], veps[:, 0, :]).then_inc(s_veps[0], 1)
            v.scalar_tensor_tensor(veps[:, 1, :], veps[:, 0, :], EPS, mv[:, :, 1], ALU.mult, ALU.add).then_inc(s_veps[0], 1)
            dve.wait_ge(s_rstd[0], 1)
            for i in range(TT):
                v.tensor_scalar(x1[:, i, :], x[:, i, :], mv[:, i, 0:1], rstd[:, 0, i:i + 1], ALU.subtract, ALU.mult).then_inc(s_x1[0], 1)
            dve.wait_ge(s_rstd[0], 2)
            for i in range(TT):
                ins = v.tensor_scalar(xn[:, i, :], x[:, i, :], mv[:, i, 0:1], rstd[:, 1, i:i + 1], ALU.subtract, ALU.mult)
            ins.then_inc(s_xn, 1)
            dve.wait_ge(s_const, 1)
            route(0)
            for i in range(TT):
                ins = v.scalar_tensor_tensor(xres[:, i, :], x1[:, i, :], wsum[:, i:i + 1], x[:, i, :], ALU.mult, ALU.add)
            done(ins)

            K = 8

            def step1(u, b):
                j = 2 * u + b
                up, k1 = active(u, b), active(u, b, 1)
                kb = earlier(u, b, 1)[1]
                if k1:
                    dve.wait_ge(s_st, j)
                    base = K * (j - 1)
                    v.scalar_tensor_tensor(nig0[:], ig, -1.0, rbuf[:, kb, IB:IB + NH].unsqueeze(1).to_broadcast([P, HV, NH]),
                                           ALU.mult, ALU.subtract).then_inc(s_cell, 1)
                    dve.wait_ge(s_cell, base + 1)
                    v.tensor_scalar(nig[:], nig0[:], EXP_MAX, None, ALU.min).then_inc(s_nig, 1)
                    v.tensor_copy(qks[:], qk).then_inc(s_cell, 1)
                    dve.wait_ge(s_cell, base + 2)
                    v.scalar_tensor_tensor(absqk[:], qks[:], -1.0, qks[:], ALU.mult, ALU.max).then_inc(s_cell, 1)
                    dve.wait_ge(s_cell, base + 3)
                    v.tensor_scalar(nrm[:], absqk[:], CELL_EPS, None, ALU.add).then_inc(s_cell, 1)
                    dve.wait_ge(s_cell, base + 4)
                    dve.wait_ge(s_eig, j)
                    v.scalar_tensor_tensor(nrm6[:], eig[:], CELL_EPS, nrm[:], ALU.add, ALU.max).then_inc(s_cell, 1)
                    dve.wait_ge(s_cell, base + 5)
                    v.reciprocal(rn[:], nrm6[:]).then_inc(s_cell, 1)
                    dve.wait_ge(s_cell, base + 6)
                    v.tensor_tensor(cc[:], qks[:], rn[:], ALU.mult).then_inc(s_cell, 1)
                    dve.wait_ge(s_cell, base + 7)
                    v.tensor_tensor(c2[:], cc[:], cc[:], ALU.mult).then_inc(s_cell, 1)
                    dve.wait_ge(s_cell, base + 8)
                    v.tensor_tensor(c2v[:], var, c2[:], ALU.mult).then_inc(s_stf, 1)
                    dve.wait_ge(s_stf, j)
                    v.tensor_scalar(c2ve[:], c2v[:], EPS, None, ALU.add).then_inc(s_c2ve, 1)
                if up:
                    dve.wait_ge(s_thc, j + 1)
                    at_least(dve, s_st, j - 1)
                    v.scalar_tensor_tensor(ca[:, b], thc[:, b], 1.0, pre[:, b], ALU.add, ALU.mult).then_inc(s_ca, 1)
                if k1:
                    dve.wait_ge(s_rh, j)
                    at_least(dve, s_sbc, j - 1)
                    v.tensor_tensor(ss[:].rearrange("p (h k) -> p h k", h=HV), cc[:], rh[:], ALU.mult).then_inc(s_ss, 1)
                if up:
                    dve.wait_ge(s_a, j + 1)
                    v.tensor_tensor(prod[:, b], A[:].rearrange("p (c t) -> p c t", c=CH), ca[:, b], ALU.mult).then_inc(s_prod, 1)
                    dve.wait_ge(s_thz, j + 1)
                    v.scalar_tensor_tensor(zz[:, b], thz[:, b], 1.0, Z[:].rearrange("p (c t) -> p c t", c=CH), ALU.add, ALU.mult).then_inc(s_zz, 1)
                if k1:
                    dve.wait_ge(s_sbT, j)
                    dve.wait_ge(s_von, j)
                    v.tensor_tensor(t1[:], SB[:].rearrange("p (c t) -> p c t", c=CH), von[:, kb], ALU.mult).then_inc(s_t1, 1)
                    dve.wait_ge(s_t1, j)
                    for c in range(CH):
                        ins = v.scalar_tensor_tensor(h1[:, c, :], ca[:, kb, c, :], rbuf[:, kb, SK + c:SK + c + 1], t1[:, c, :], ALU.mult, ALU.add)
                    ins.then_inc(s_h1, 1)
                    dve.wait_ge(s_h1, j)
                    at_least(dve, s_y[0], j - 2)
                    v.tensor_tensor(hs[:, kb], h1[:], zz[:, kb], ALU.mult).then_inc(s_hs, 1)
            steps(dve, step1, 1)

            def combine(l, c):
                cols = range(c * TT // 4, (c + 1) * TT // 4)
                dve.wait_ge(s_yin[l][c], 16)
                for k in range(TOPK):
                    for i in cols:
                        ins = v.scalar_tensor_tensor(xres[:, i, :], ypair[:, TOPK * i + k, :], wh[l][:, i, k:k + 1], xres[:, i, :], ALU.mult, ALU.add)
                    if k == 0:
                        done(ins)
                return ins, cols

            for c in range(4):
                ins, cols = combine(0, c)
                done(ins)
                ins = stats(xres, cols)
            done(ins)
            v.tensor_scalar(veps[:, 0, :], mv[:, :, 1], EPS, None, ALU.add).then_inc(s_veps[1], 1)
            dve.wait_ge(s_rstd[1], 1)
            for i in range(TT):
                ins = v.tensor_scalar(x1[:, i, :], xres[:, i, :], mv[:, i, 0:1], rstd[:, 0, i:i + 1], ALU.subtract, ALU.mult)
            ins.then_inc(s_x1[1], 1)
            route(1)

            def step2(u, b):
                if not active(u, b):
                    return
                j = 2 * u + b
                dve.wait_ge(s_thg, j + 1)
                v.scalar_tensor_tensor(ca[:, b], thc[:, b], 1.0, bank[2 + b][:].rearrange("p (c t) -> p c t", c=CH), ALU.add, ALU.mult).then_inc(s_gg, 1)
                dve.wait_ge(s_gg, j + 1)
                dve.wait_ge(s_u, j + 1)
                at_least(dve, s_y[1], j - 1)
                v.tensor_tensor(hs[:, b], bank[4 + b][:].rearrange("p (c t) -> p c t", c=CH), ca[:, b], ALU.mult).then_inc(s_hh, 1)
            steps(dve, step2, 0)
            for c in range(4):
                combine(1, c)[0].then_inc(s_out, 1)


_INS = ["hidden_states", "gate_w", "ln_w", "w_up", "conv_w", "conv_b", "q_w", "k_w", "v_w", "ig_w", "ig_b",
        "on_w", "skip_w", "w_down"]
_FFN = ["router_w", "w_gate", "w_up", "w_down"]


def kernel(**inputs):
    import numpy as _np
    import concourse.bacc as _bacc
    from concourse import mybir as _mybir
    from concourse.bass_utils import run_bass_kernel_spmd as _run

    nc = _bacc.Bacc("TRN2", target_bir_lowering=False, num_devices=1)
    arrays, args = {}, []
    for name in ["L0_attn_" + n for n in _INS] + ["L0_ffn_" + n for n in _FFN]:
        a = _np.ascontiguousarray(inputs[name])
        arrays[f"in_{name}"] = a
        args.append(nc.dram_tensor(f"in_{name}", a.shape, _mybir.dt.from_np(a.dtype), kind="ExternalInput").ap())
    args.append(nc.dram_tensor("out_0", inputs["L0_attn_hidden_states"].shape, _mybir.dt.float32, kind="ExternalOutput").ap())
    program(nc, *args)
    return _run(nc, [arrays], core_ids=[0]).results[0]["out_0"]
```

```python
from contextlib import ExitStack

import concourse.bass as bass
from concourse import mybir

ALU = mybir.AluOpType
ACT = mybir.ActivationFunctionType
F32 = mybir.dt.float32
BF16 = mybir.dt.bfloat16
I32 = mybir.dt.int32
U32 = mybir.dt.uint32
AXX = mybir.AxisListType.X

P = 128
NTOK, D = 2048, 128
TT = NTOK // P
E, TOPK = 8, 2
I = 256
CH = I // P
NH, QB = 4, 4
DH = I // NH
NB = P // QB
TS = 256
HV = TS // P
NT = (TOPK * NTOK + E * (TS - 1)) // TS
NA = NT * HV
NP = NT // 2
PAIRS = TOPK * NTOK
EPS = 1e-5
CELL_EPS = 1e-6
EXP_MAX = 85.0
assert NT % 2 == 1 and NA <= P and P * 2 * TT == PAIRS

WC, WZ, KQ, WV = 0, I, 2 * I, 3 * I
GX, GC = 4 * I, 4 * I + NH
CB, SK, ON = GC + CH * NH, GC + CH * NH + CH, GC + CH * NH + 2 * CH
IB = ON + CH
REC = IB + NH


def at_least(eng, sem, value):
    if not isinstance(value, int) or value > 0:
        eng.wait_ge(sem, value)


def program(nc, hidden, gate_w, ln_w, w_up, conv_w, conv_b, q_w, k_w, v_w, ig_w, ig_b, on_w,
            skip_w, w_down, router_w, f_gate, f_up, f_down, out):
    with ExitStack() as ctx:
        def sb(name, shape, dt=F32):
            return ctx.enter_context(nc.sbuf_tensor(name, shape, dt))

        def sem(name):
            return ctx.enter_context(nc.semaphore(name))

        bank = [ctx.enter_context(nc.psum_tensor(f"bank{i}", [P, 512], F32)) for i in range(8)]

        xrows = [nc.dram_tensor(f"xrows{l}", [NTOK, D], F32, kind="Internal").ap() for l in range(2)]
        yrows = [nc.dram_tensor(f"yrows{l}", [PAIRS + NT * TS, D], F32, kind="Internal").ap() for l in range(2)]

        ident = sb("ident", [P, P])
        lower = sb("lower", [P, P], BF16)
        ones = sb("ones", [P, P], BF16)
        iota_p = sb("iota_p", [P, P], BF16)
        iota_a = sb("iota_a", [P, NA])
        part = sb("part", [P, 1])
        pairno = sb("pairno", [P, TT * TOPK])
        spare = sb("spare", [P, NA])
        ekey = sb("ekey", [P, E])
        tilecut = sb("tilecut", [P, E])
        upto = sb("upto", [P, E, E])
        tileno = sb("tileno", [P, NT + 1])
        blockmask = sb("blockmask", [P, NB])
        headmask = sb("headmask", [P, 2])
        centre = sb("centre", [P, P])
        headsum = sb("headsum", [P, CH, NH])
        neghalf = sb("neghalf", [P, TT])

        x = sb("x", [P, TT, D])
        x1 = sb("x1", [P, TT, D])
        xn = sb("xn", [P, TT, D])
        xres = x
        x1T = sb("x1T", [P, TT, P])
        bn = sb("bn", [P, TT, 6])
        mv = sb("mv", [P, TT, 2])
        veps = sb("veps", [P, 2, TT])
        rstd = sb("rstd", [P, 2, TT])
        shift = sb("shift", [P, TT])

        lg = sb("lg", [P, TT, E])
        key = sb("key", [P, TT, E])
        top = sb("top", [P, TT, TOPK])
        kmax = sb("kmax", [P, TT])
        pick = sb("pick", [P, TT, TOPK, E])
        picked = sb("picked", [P, TT + 1, E], BF16)
        cmp8 = sb("cmp8", [P, E, E])
        ntile = sb("ntile", [P, E])
        cum = sb("cum", [P, E])
        before = sb("before", [P, E])
        place = sb("place", [P, TT, E])
        pslot = sb("pslot", [P, TT, TOPK, E])
        slot = sb("slot", [P, TT * TOPK])
        sloti = sb("sloti", [P, TT * TOPK], I32)
        loi = sb("loi", [P, TT * TOPK], I32)
        hii = sb("hii", [P, TT * TOPK], I32)
        lof = sb("lof", [P, TT * TOPK])
        hif = sb("hif", [P, TT * TOPK])
        cmpj = sb("cmpj", [1, NT + 1, E])
        ej = sb("ej", [1, NT + 1])
        expert = [sb(f"expert{l}", [1, NT + 1], I32) for l in range(2)]
        onehot = sb("onehot", [P, TT * TOPK, P], BF16)
        rhs = sb("rhs", [P, TT * TOPK, 3 * NA], BF16)
        perm = sb("perm", [P, 3 * NA])
        pairf = sb("pairf", [P, NA])
        unused = sb("unused", [P, NA])
        pairi = sb("pairi", [P, NA], U32)
        gidx = [sb(f"gidx{l}", [P, NA], U32) for l in range(2)]
        sidx = [sb(f"sidx{l}", [P, NA], U32) for l in range(2)]
        ex = sb("ex", [P, TT, TOPK])
        den = sb("den", [P, TT, TOPK])
        wt = sb("wt", [P, TT, TOPK])
        wsum = sb("wsum", [P, TT])
        wh = [sb(f"wh{l}", [P, TT, TOPK]) for l in range(2)]

        raw1 = sb("raw1", [64, 4 * P])
        raw2 = sb("raw2", [48, 4 * P])
        raw3 = sb("raw3", [64, P])
        gate = sb("gate", [P, E])
        qkvT = sb("qkvT", [P, QB, 64])
        igT = sb("igT", [P, NH, 48])
        parT = sb("parT", [P, 64])
        wraw = sb("wraw", [P, E, 2 * I])
        blocks = sb("blocks", [P, 3 * E * CH, P + NH])
        cig = sb("cig", [P, 2, CH, P + NH])
        mT = sb("mT", [P, 2, CH, P])
        mTs = sb("mTs", [P, 2, CH, P])
        vT = sb("vT", [P, 2, CH, P + NH])
        rec = sb("rec", [P, E, REC])
        wd1 = sb("wd1", [P, E, CH, D])
        gu = sb("gu", [P, E, 2, I])
        wd2 = sb("wd2", [P, E, CH, D])
        ypair = blocks[:, 0:2 * E * CH, 0:D]

        gi = sb("gi", [P, 2, HV], U32)
        si = sb("si", [P, 2, HV], U32)
        rbuf = sb("rbuf", [P, 2, REC])
        gubuf = rbuf[:, :, 0:2 * I].rearrange("p b (g n) -> p b g n", g=2)
        wdbuf = sb("wdbuf", [P, 2, CH, D])
        xg = sb("xg", [P, 2, HV, D])
        xT = sb("xT", [P, 2, TS])
        pre = sb("pre", [P, 2, CH, TS])
        def tiles(buf, n):
            return buf[:].rearrange("p a b -> p (a b)")[:, n * 2 * I * 2:(n + 1) * 2 * I * 2]\
                .rearrange("p (b c t) -> p b c t", b=2, c=CH)

        thc, thz = tiles(xn, 0), tiles(xn, 1)
        sq, hs = tiles(x1T, 0)[:, 0], tiles(x1T, 1)
        ca, zz, cask, prod = (tiles(wraw, n) for n in range(4))
        vs = sb("vs", [P, HV, I])
        h1 = sb("h1", [P, CH, TS])
        onib = sb("onib", [P, 2, CH + NH])
        yb = sb("yb", [P, 2, HV, D])
        nig0 = sb("nig0", [P, HV, NH])
        nig = sb("nig", [P, HV, NH])
        eig = sb("eig", [P, HV, NH])
        qks = sb("qks", [P, HV, NH])
        absqk = sb("absqk", [P, HV, NH])
        nrm6 = sb("nrm6", [P, HV, NH])
        abs6 = sb("abs6", [P, HV, NH])
        rn = sb("rn", [P, HV, NH])
        cc = sb("cc", [P, HV, NH])
        c2 = sb("c2", [P, HV, NH])
        var = sb("var", [P, 2, HV, NH])
        c2v = sb("c2v", [P, HV, NH])
        c2ve = sb("c2ve", [P, HV, NH])
        rh = sb("rh", [P, HV, NH])
        ss = sb("ss", [P, HV * NH])

        s_x, s_raw, s_gate, s_wraw, s_ib, s_late = (sem(n) for n in (
            "x_loaded", "raw_loaded", "gate_loaded", "wup_loaded", "igb_loaded", "late_loaded"))
        s_pool = sem("pool_step")
        s_const = sem("consts_ready")
        s_dve = sem("dve_step")
        s_veps = [sem(f"veps_ready{l}") for l in range(2)]
        s_rstd = [sem(f"rstd_ready{l}") for l in range(2)]
        s_x1 = [sem(f"normed_ready{l}") for l in range(2)]
        s_xn = sem("xn_ready")
        s_shift = sem("shift_ready")
        s_x1T = [sem(f"normedT_psum{l}") for l in range(2)]
        s_x1Tc = [sem(f"normedT_copied{l}") for l in range(2)]
        s_lg = [sem(f"logits_ready{l}") for l in range(2)]
        s_top = [sem(f"top_ready{l}") for l in range(2)]
        s_ex = [sem(f"topexp_ready{l}") for l in range(2)]
        s_picked = [sem(f"picked_ready{l}") for l in range(2)]
        s_rank = [sem(f"rank_ready{l}") for l in range(2)]
        s_hot = [sem(f"onehots_ready{l}") for l in range(2)]
        s_perm = [sem(f"perm_ready{l}") for l in range(2)]
        s_idx = [sem(f"indices_ready{l}") for l in range(2)]
        s_exp = [sem(f"experts_ready{l}") for l in range(2)]
        s_rows = [sem(f"xrows_stored{l}") for l in range(2)]
        s_parp, s_parT, s_wl = sem("par_psum"), sem("par_copied"), sem("wl_ready")
        s_blk = [sem(f"blocks_ready{m}") for m in "qkv"]
        s_wz = sem("wz_ready")
        s_cig = sem("cig_ready")
        s_pT, s_pV, s_pKQ, s_pWc, s_pWv = (sem(n) for n in ("mT_psum", "vT_psum", "kq_psum", "wc_psum", "wv_psum"))
        s_mT, s_vT, s_kq, s_wc, s_rec = (sem(n) for n in ("mT_copied", "vT_copied", "kq_copied", "wc_copied", "record_ready"))
        s_par2 = sem("params_in_record")
        s_gath = [[sem(f"gathered{l}{b}") for b in range(2)] for l in range(2)]
        s_scat = [[sem(f"scattered{l}{b}") for b in range(2)] for l in range(2)]
        s_wbuf = [[sem(f"weights_in{l}{b}") for b in range(2)] for l in range(2)]
        s_wdbuf = [[sem(f"wdown_in{l}{b}") for b in range(2)] for l in range(2)]
        s_gi = [sem(f"gi_copied{l}") for l in range(2)]
        s_issue = sem("pool_issues")
        s_si = [sem(f"si_copied{l}") for l in range(2)]
        s_xtp = [sem(f"xT_psum{l}") for l in range(2)]
        s_xts = [sem(f"xT_copied{l}") for l in range(2)]
        s_y = [sem(f"y_psum{l}") for l in range(2)]
        s_yb = [sem(f"y_copied{l}") for l in range(2)]
        s_pc, s_vc, s_z, s_a, s_st, s_vt = (sem(n) for n in (
            "conv_psum", "v_psum", "z_psum", "kqca_psum", "stats_psum", "vT_tile_psum"))
        s_pre, s_thc, s_cask, s_thz, s_eig = (sem(n) for n in (
            "pre_ready", "tanh_conv", "skip_ready", "tanh_z", "exp_ig"))
        s_nig, s_cell, s_stf, s_var, s_c2v, s_c2ve, s_rh, s_ss = (sem(n) for n in (
            "nig_ready", "cell_step", "stats_read", "var_ready", "c2v_ready", "c2ve_ready", "rstd_h", "scale_ready"))
        s_onib, s_ca, s_prod, s_zz, s_vs, s_h1, s_hs = (sem(n) for n in (
            "onib_copied", "ca_ready", "prod_ready", "zz_ready", "vs_ready", "h1_ready", "hs_ready"))
        s_g, s_u, s_thg, s_gg, s_hh = (sem(n) for n in (
            "gate_psum", "up_psum", "tanh_gate", "gated", "ffn_h"))
        s_yin = [[sem(f"ypair_loaded{l}{c}") for c in range(4)] for l in range(2)]
        s_out = sem("out_ready")
        s_st_out = sem("out_stored")

        out_v = out.rearrange("b s d -> (b s) d").rearrange("(p i) d -> p i d", i=TT)
        x_v = hidden.rearrange("b s d -> (b s) d").rearrange("(p i) d -> p i d", i=TT)
        Lp, Rp, Mp = bank[7][:, 0:TT * E], bank[7][:, 128:128 + (TT + 1) * E], bank[7][:, 288:288 + 3 * NA][:, 0:138]
        Mp = bank[5][:, 0:3 * NA]
        XT, PC, VC, Z, A, ST, Y = bank[0], bank[1], bank[2:4], bank[4], bank[5], bank[6], bank[7]
        VT = XT
        qk = ST[:, 0:HV * 8].rearrange("p (h k) -> p h k", h=HV)[:, :, 0:4]
        ig = ST[:, 0:HV * 8].rearrange("p (h k) -> p h k", h=HV)[:, :, 4:8]

        last0, last1 = (NT + 1) // 2, NT // 2
        block = ctx.enter_context(nc.Block())

        def steps(eng, step, lag, head=1):
            for j in range(2 * head):
                step(j // 2, j % 2)
            with eng.Fori(head, NP - 1) as u:
                for b in range(2):
                    step(u, b)
            for j in range(2 * (NP - 1), NT + lag):
                step(j // 2, j % 2)

        def active(u, b, back=0):
            return not isinstance(u, int) or 0 <= 2 * u + b - back < NT

        def earlier(u, b, back):
            return (u - (back - b + 1) // 2, (b - back) % 2)

        @block.sync
        def _(sp):
            h = TT // 2
            sp.dma_start(x[:, 0:h, :], x_v[:, 0:h, :]).then_inc(s_x, 16)
            sp.dma_start(x[:, h:TT, :], x_v[:, h:TT, :]).then_inc(s_x, 16)
            sp.dma_start(gate[:], gate_w).then_inc(s_gate, 16)
            sp.dma_start(wraw[:], w_up.rearrange("e d n -> d e n")).then_inc(s_wraw, 16)
            sp.wait_ge(s_raw, 16 * 10)
            sp.dma_start(wd1[:], w_down.rearrange("e (c p) d -> p e c d", p=P)).then_inc(s_late, 16)
            sp.dma_start(gu[:, :, 0, :], f_gate.rearrange("e d n -> d e n")).then_inc(s_late, 16)
            sp.dma_start(gu[:, :, 1, :], f_up.rearrange("e d n -> d e n")).then_inc(s_late, 16)
            sp.dma_start(wd2[:], f_down.rearrange("e (c p) d -> p e c d", p=P)).then_inc(s_late, 16)

            sp.wait_ge(s_xn, 1)
            sp.dma_start(xrows[0].rearrange("(p i) d -> p i d", i=TT), xn[:]).then_inc(s_rows[0], 16)

            sp.wait_ge(s_exp[0], 1)
            sp.wait_ge(s_rec, E)
            sp.wait_ge(s_par2, 4)
            sp.wait_ge(s_kq, 2 * E)
            sp.wait_ge(s_wc, E)
            sp.wait_ge(s_wz, E)
            sp.wait_ge(s_late, 64)

            def load_expert(l, u, b, body):
                if active(u, b):
                    body(sp.value_load(expert[l][0:1, bass.ds(2 * u + b, 1)], min_val=0, max_val=E - 1))

            def load_down(l, u, b, wd):
                def body(e):
                    at_least(sp, s_y[l], 2 * u + b - 1)
                    sp.dma_start(wdbuf[:, b], wd[:, bass.ds(e, 1), :, :].rearrange("p a c d -> p (a c) d"))\
                        .then_inc(s_wdbuf[l][b], 16)
                load_expert(l, u, b, body)

            def load1(u, b):
                def body(e):
                    j = 2 * u + b
                    at_least(sp, s_z, j - 1)
                    at_least(sp, s_cask, j - 1)
                    at_least(sp, s_onib, j - 1)
                    sp.dma_start(rbuf[:, b, :], rec[:, bass.ds(e, 1), :].rearrange("p a n -> p (a n)"))\
                        .then_inc(s_wbuf[0][b], 16)
                load_expert(0, u, b, body)
                load_down(0, *earlier(u, b, 1), wd1)
            steps(sp, load1, 1)

            def load_pairs(l):
                sp.wait_ge(s_scat[l][0], 32 * last0)
                sp.wait_ge(s_scat[l][1], 32 * last1)
                yv = yrows[l][0:PAIRS, :].rearrange("(p m) d -> p m d", p=P)
                for c in range(4):
                    m = PAIRS // P // 4
                    sp.dma_start(ypair[:, c * m:(c + 1) * m, :], yv[:, c * m:(c + 1) * m, :])\
                        .then_inc(s_yin[l][c], 16)
            load_pairs(0)

            sp.wait_ge(s_x1[1], 1)
            sp.dma_start(xrows[1].rearrange("(p i) d -> p i d", i=TT), x1[:]).then_inc(s_rows[1], 16)
            sp.wait_ge(s_exp[1], 1)
            sp.wait_ge(s_late, 64)

            def load2(u, b):
                def body(e):
                    at_least(sp, s_u, 2 * u + b - 1)
                    sp.dma_start(gubuf[:, b, :, :], gu[:, bass.ds(e, 1), :, :].rearrange("p a g n -> p (a g) n"))\
                        .then_inc(s_wbuf[1][b], 16)
                load_expert(1, u, b, body)
                load_down(1, u, b, wd2)
            steps(sp, load2, 0)
            load_pairs(1)
            for c in range(4):
                m = TT // 4
                sp.wait_ge(s_out, c + 1)
                sp.dma_start(out_v[:, c * m:(c + 1) * m, :], xres[:, c * m:(c + 1) * m, :])\
                    .then_inc(s_st_out, 16)
            sp.wait_ge(s_st_out, 64)

        def spread_blocks(eng, m):
            n = E * CH
            eng.tensor_tensor(
                blocks[:, m * n:(m + 1) * n, 0:P].rearrange("p m (n b) -> p m n b", b=QB),
                blockmask[:][:, None, :, None].to_broadcast([P, n, NB, QB]),
                qkvT[:, :, m * n:(m + 1) * n].rearrange("p b m -> p m b").unsqueeze(2).to_broadcast([P, n, NB, QB]),
                ALU.mult).then_inc(s_blk[m], 1)
            if m == 0:
                eng.tensor_copy(blocks[:, 0:n, P:].rearrange("p (e c) h -> p e c h", c=CH),
                                igT[:].rearrange("p h (e s) -> p e s h", e=E)[:, :, CH:2 * CH, :]).then_inc(s_blk[m], 1)

        @block.gpsimd
        def _(pool):
            g = nc.gpsimd
            count = [0]

            def done(ins):
                count[0] += 1
                ins.then_inc(s_pool, 1)
                pool.wait_ge(s_pool, count[0])

            def select(t, pattern, base, cm, op=ALU.is_ge):
                done(g.affine_select(out=t, in_=t, compare_op=op, fill=0.0, base=base,
                                     pattern=pattern, channel_multiplier=cm))

            done(g.memset(ident[:], 0.0))
            done(g.affine_select(out=ident[:], in_=ident[:], compare_op=ALU.not_equal, fill=1.0, base=0,
                                 pattern=[[-1, P]], channel_multiplier=1))
            g.memset(picked[:], 0.0)
            g.memset(neghalf[:], -0.5)
            done(g.memset(blockmask[:], 1.0))
            select(blockmask[:], [[-QB, NB]], 0, 1)
            select(blockmask[:], [[QB, NB]], QB - 1, -1)
            done(g.memset(headmask[:], 1.0))
            select(headmask[:], [[-DH, 2]], 0, 1)
            select(headmask[:], [[DH, 2]], DH - 1, -1)
            done(g.memset(headsum[:], 0.0))
            for c in range(CH):
                g.tensor_scalar(headsum[:, c, 2 * c:2 * c + 2], headmask[:], DH ** -0.5 / 4, None, ALU.mult)
            done(g.tensor_scalar(centre[:].rearrange("p (k r) -> p k r", k=2),
                                 headmask[:].unsqueeze(2).to_broadcast([P, 2, DH]), -1.0 / DH, None, ALU.mult))
            done(g.tensor_tensor(centre[:], centre[:], ident[:], ALU.add))
            for p in range(2):
                g.tensor_copy(cig[:, p, 0, 0:P], centre[:])
                g.tensor_copy(cig[:, p, 1, NH:], centre[:])
            small = dict(allow_small_or_imprecise_dtypes=True)
            done(g.iota(ekey[:], pattern=[[-1, E]], base=E, channel_multiplier=0, **small))
            done(g.memset(lower[:], 1.0))
            select(lower[:], [[1, P]], -1, -1)
            g.memset(ones[:], 1.0)
            done(g.memset(upto[:], 1.0))
            select(upto[:], [[1, E], [-1, E]], 0, 0)
            g.iota(tilecut[:], pattern=[[TS, E]], base=0, channel_multiplier=0, **small)
            g.iota(tileno[:], pattern=[[1, NT + 1]], base=0, channel_multiplier=0, **small)
            g.iota(iota_p[:], pattern=[[1, P]], base=0, channel_multiplier=0, **small)
            g.iota(iota_a[:], pattern=[[1, NA]], base=0, channel_multiplier=0, **small)
            g.iota(part[:], pattern=[[0, 1]], base=0, channel_multiplier=1, **small)
            g.iota(pairno[:], pattern=[[1, TT * TOPK]], base=0, channel_multiplier=0, **small)
            done(g.iota(spare[:], pattern=[[P, NA]], base=PAIRS, channel_multiplier=1, **small))
            g.memset(cmpj[:], 0.0).then_inc(s_const, 1)

            for k in range(2):
                pool.wait_ge(s_veps[0], k + 1)
                g.tensor_tensor(rstd[:, k, :], veps[:, k, :], neghalf[:], ALU.pow).then_inc(s_rstd[0], 1)

            pool.wait_ge(s_parT, 1)
            pool.wait_ge(s_wraw, 16)
            at = 3 * E * CH

            def fold(e):
                w = parT[:, at + e:at + e + 1]
                g.tensor_scalar(wraw[:, e, 0:I], wraw[:, e, 0:I], w, None, ALU.mult).then_inc(s_wl, 1)
                g.tensor_scalar(rec[:, e, WZ:WZ + I], wraw[:, e, I:2 * I], w, None, ALU.mult).then_inc(s_wz, 1)
                if e >= 2:
                    pool.wait_ge(s_pV, e - 1)
                g.tensor_copy(cig[:, e % 2].rearrange("p c n -> p (c n)")[:, P:P + CH * NH].rearrange("p (c h) -> p c h", c=CH),
                              igT[:, :, 6 * e + 2 * CH:6 * e + 3 * CH].rearrange("p h c -> p c h")).then_inc(s_cig, 1)

            for e in range(2):
                fold(e)
            spread_blocks(g, 2)
            for e in range(2, E):
                fold(e)

            def gather(l, u, b, used):
                if not active(u, b):
                    return
                j = 2 * u + b
                col = pool.snap(HV * j)
                at_least(pool, used, j - 1)
                g.tensor_copy(gi[:, b, :], gidx[l][:, bass.ds(col, HV)]).then_inc(s_gi[l], 1)
                pool.wait_ge(s_rows[l], 16)
                pool.wait_ge(s_gi[l], j + 1)
                pool.sem_inc(s_issue, 1)
                for h in range(HV):
                    g.indirect_dma_start(
                        xg[:, b, h, :], None, xrows[l], bass.IndirectOffsetOnAxis(ap=gi[:, b, h:h + 1], axis=0)).then_inc(s_gath[l][b], 16)

            def scatter(l, u, b):
                if not active(u, b):
                    return
                j = 2 * u + b
                col = pool.snap(HV * j)
                at_least(pool, s_scat[l][b], 32 * u)
                g.tensor_copy(si[:, b, :], sidx[l][:, bass.ds(col, HV)]).then_inc(s_si[l], 1)
                pool.wait_ge(s_si[l], j + 1)
                pool.wait_ge(s_yb[l], j + 1)
                pool.sem_inc(s_issue, 1)
                for h in range(HV):
                    g.indirect_dma_start(
                        yrows[l], bass.IndirectOffsetOnAxis(ap=si[:, b, h:h + 1], axis=0), yb[:, b, h, :], None).then_inc(s_scat[l][b], 16)

            pool.wait_ge(s_idx[0], 1)
            for b in range(2):
                gather(0, 0, b, s_xtp[0])

            def step1(u, b):
                k, kb = earlier(u, b, 1)
                if active(k, kb):
                    pool.wait_ge(s_c2ve, 2 * k + kb + 1)
                    at_least(pool, s_ss, 2 * k + kb)
                    g.tensor_tensor(rh[:], c2ve[:], neghalf[:, 0:HV * NH].rearrange("p (h k) -> p h k", h=HV),
                                    ALU.pow).then_inc(s_rh, 1)
                gather(0, *earlier(u, b, -2), s_xtp[0])
                scatter(0, *earlier(u, b, 2))
            steps(pool, step1, 2)

            pool.wait_ge(s_veps[1], 1)
            g.tensor_tensor(rstd[:, 0, :], veps[:, 0, :], neghalf[:], ALU.pow).then_inc(s_rstd[1], 1)
            pool.wait_ge(s_idx[1], 1)
            for b in range(2):
                gather(1, 0, b, s_xtp[1])

            def step2(u, b):
                gather(1, *earlier(u, b, -2), s_xtp[1])
                scatter(1, *earlier(u, b, 1))
            steps(pool, step2, 1)

        @block.scalar
        def _(act):
            a = nc.scalar
            r = E * CH
            for m, w in enumerate((q_w, k_w, v_w)):
                act.dma_start(raw1[m * r:(m + 1) * r, :], w.rearrange("e (c n) o b -> (e c) (n o b)", c=CH)).then_inc(s_raw, 16)
            act.dma_start(raw1[3 * r:4 * r, :], conv_w.rearrange("e (c p) k -> (e c) (p k)", c=CH)).then_inc(s_raw, 16)
            act.dma_start(raw2[:], ig_w.rearrange("e (s p) h -> (e s) (p h)", p=P)).then_inc(s_raw, 16)
            for m, w in enumerate((conv_b, on_w, skip_w)):
                act.dma_start(raw3[m * r:(m + 1) * r, :], w.rearrange("e (c p) -> (e c) p", c=CH)).then_inc(s_raw, 16)
            act.dma_start(raw3[3 * r:3 * r + E, :], ln_w).then_inc(s_raw, 16)
            act.dma_start(raw3[3 * r + E:3 * r + 2 * E, :], router_w).then_inc(s_raw, 16)
            act.dma_start(rec[:, :, IB:IB + NH], ig_b.unsqueeze(0).to_broadcast([P, E, NH])).then_inc(s_ib, 16)

            act.wait_ge(s_parp, 1)
            a.activation(qkvT[:].rearrange("p b m -> p (b m)"), bank[0][:, 0:4 * 64], ACT.Copy)
            a.activation(igT[:].rearrange("p h m -> p (h m)"), bank[1][:, 0:4 * 48], ACT.Copy)
            a.activation(parT[:], bank[2][:, 0:64], ACT.Copy).then_inc(s_parT, 1)
            act.wait_ge(s_parT, 1)
            act.wait_ge(s_ib, 16)
            for m, (col, scale) in enumerate(((CB, 1.0), (ON, 1.0), (SK, 0.5))):
                a.activation(rec[:, :, col:col + CH], parT[:, m * r:(m + 1) * r].rearrange("p (e c) -> p e c", c=CH),
                             ACT.Copy, scale=scale).then_inc(s_par2, 1)

            def transposed(l):
                for q in range(4):
                    act.wait_ge(s_x1T[l], q + 1)
                    a.activation(x1T[:, 4 * q:4 * q + 4, :].rearrange("p i t -> p (i t)"), bank[5 + q % 2][:, :],
                                 ACT.Copy).then_inc(s_x1Tc[l], 1)

            def prepare1(e):
                p = e % 2
                act.wait_ge(s_pT, e + 1)
                if e >= 2:
                    act.wait_ge(s_pWv, e - 1)
                a.activation(mT[:, p].rearrange("p c t -> p (c t)"), bank[0][:, 0:I], ACT.Copy)
                for c in range(CH):
                    at = 3 * r + e * CH + c
                    a.activation(mTs[:, p, c, :], bank[0][:, c * P:(c + 1) * P], ACT.Copy,
                                 scale=qkvT[:, 3, at:at + 1]).then_inc(s_mT, 1)
                act.wait_ge(s_pV, e + 1)
                a.activation(vT[:, p].rearrange("p c t -> p (c t)"), bank[1][:, 0:CH * (P + NH)], ACT.Copy).then_inc(s_vT, 1)
                act.wait_ge(s_pKQ, e + 1)
                kq = bank[2][:, 0:CH * (P + NH)].rearrange("p (c n) -> p c n", c=CH)
                a.activation(rec[:, e, KQ:KQ + I].rearrange("p (c n) -> p c n", c=CH), kq[:, :, 0:P], ACT.Copy).then_inc(s_kq, 1)
                a.activation(rec[:, e, GC:GC + CH * NH].rearrange("p (c h) -> p c h", c=CH), kq[:, :, P:], ACT.Copy, scale=0.5).then_inc(s_kq, 1)

            def prepare2(e):
                act.wait_ge(s_pWc, e + 1)
                a.activation(rec[:, e, WC:WC + I], bank[3][:, 0:I], ACT.Copy).then_inc(s_wc, 1)
                act.wait_ge(s_pWv, e + 1)
                a.activation(rec[:, e, WV:WV + I].rearrange("p (c n) -> p c n", c=CH),
                             bank[4][:, 0:CH * (P + NH)].rearrange("p (c n) -> p c n", c=CH)[:, :, 0:P], ACT.Copy)
                a.activation(rec[:, e, GX:GX + NH], bank[4][:, P:P + NH], ACT.Copy).then_inc(s_rec, 1)

            transposed(0)
            act.wait_ge(s_shift, 1)
            for i in range(TT):
                ins = a.activation(xn[:, i, :], x[:, i, :], ACT.Identity, bias=shift[:, i:i + 1], scale=rstd[:, 1, i:i + 1])
            ins.then_inc(s_xn, 1)
            for e in range(E):
                prepare1(e)
                if e:
                    prepare2(e - 1)
                if e == 3:
                    act.wait_ge(s_top[0], 1)
                    a.activation(ex[:, :, 0], den[:, :, 0], ACT.Exp).then_inc(s_ex[0], 1)
            prepare2(E - 1)
            act.wait_ge(s_par2, 3)
            act.wait_ge(s_rec, E)
            a.activation(neghalf[:, 0:1], neghalf[:, 0:1], ACT.Copy).then_inc(s_par2, 1)

            def in_copy1(u, b):
                if not active(u, b):
                    return
                j = 2 * u + b
                act.wait_ge(s_xtp[0], j + 1)
                at_least(act, s_z, j - 1)
                a.activation(xT[:, b, :], XT[:, 0:TS], ACT.Copy).then_inc(s_xts[0], 1)

            def step1(u, b):
                j = 2 * u + b
                up, k1, k2 = active(u, b), active(u, b, 1), active(u, b, 2)
                if k1:
                    act.wait_ge(s_nig, j)
                    a.activation(eig[:], nig[:], ACT.Exp).then_inc(s_eig, 1)
                if up:
                    act.wait_ge(s_pc, j + 1)
                    act.wait_ge(s_wbuf[0][b], 16 * (u + 1))
                    at_least(act, s_ca, CH * (j - 1))
                    for c in range(CH):
                        a.activation(pre[:, b, c, :], PC[:, c * TS:(c + 1) * TS], ACT.Identity,
                                     bias=rbuf[:, b, CB + c:CB + c + 1]).then_inc(s_pre, 1)
                    act.wait_ge(s_pre, 2 * j + 2)
                    a.activation(thc[:, b], pre[:, b], ACT.Tanh, scale=0.5).then_inc(s_thc, 1)
                if k2:
                    y_out(0, *earlier(u, b, 2), Y)
                if up:
                    act.wait_ge(s_vc, j + 1)
                    at_least(act, s_c2v, j - 1)
                    for h in range(HV):
                        for k in range(NH):
                            o = h * I + k * DH
                            ins = a.activation(sq[:, h, k * DH:(k + 1) * DH], VC[b][:, o:o + DH], ACT.Square, scale=DH ** -0.5,
                                               accum_out=var[:, b, h, k:k + 1])
                    ins.then_inc(s_var, 1)
                    in_copy1(*earlier(u, b, -1))
                    act.wait_ge(s_ca, CH * (j + 1))
                    at_least(act, s_h1, j - 1)
                    for c in range(CH):
                        ins = a.activation(cask[:, b, c, :], ca[:, b, c, :], ACT.Copy,
                                           scale=rbuf[:, b, SK + c:SK + c + 1])
                    ins.then_inc(s_cask, 1)
                    act.wait_ge(s_z, j + 1)
                    at_least(act, s_zz, j - 1)
                    a.activation(thz[:, b], Z[:].rearrange("p (c t) -> p c t", c=CH), ACT.Tanh, scale=0.5).then_inc(s_thz, 1)

            def y_out(l, k, kb, src):
                act.wait_ge(s_y[l], 2 * k + kb + 1)
                at_least(act, s_scat[l][kb], 32 * k)
                a.activation(yb[:, kb], src[:, 0:TS].rearrange("p (h d) -> p h d", h=HV), ACT.Copy).then_inc(s_yb[l], 1)
            in_copy1(0, 0)
            steps(act, step1, 2)

            transposed(1)
            act.wait_ge(s_top[1], 1)
            a.activation(ex[:], den[:], ACT.Exp, scale=-1.0).then_inc(s_ex[1], 1)

            def step2(u, b):
                j = 2 * u + b
                if active(u, b):
                    act.wait_ge(s_xtp[1], j + 1)
                    a.activation(xT[:, b, :], bank[b][:, 0:TS], ACT.Copy).then_inc(s_xts[1], 1)
                    act.wait_ge(s_g, j + 1)
                    at_least(act, s_gg, j - 1)
                    a.activation(thc[:, b], bank[2 + b][:].rearrange("p (c t) -> p c t", c=CH), ACT.Tanh, scale=0.5).then_inc(s_thg, 1)
                if active(u, b, 1):
                    k, kb = earlier(u, b, 1)
                    y_out(1, k, kb, bank[6 + kb])
            steps(act, step2, 1)

        @block.tensor
        def _(pe):
            t = nc.tensor
            r = E * CH
            pe.wait_ge(s_pool, 2)
            pe.wait_ge(s_raw, 16 * 10)
            for b in range(QB):
                t.transpose(bank[0][:, b * 64:(b + 1) * 64], raw1[:, b:4 * P:4], ident[0:64, 0:64])
            for h in range(NH):
                t.transpose(bank[1][:, h * 48:(h + 1) * 48], raw2[:, h:4 * P:4], ident[0:48, 0:48])
            t.transpose(bank[2][:, 0:64], raw3[:], ident[0:64, 0:64]).then_inc(s_parp, 1)

            def route_transposes(l):
                for q in range(4):
                    if l == 0:
                        pe.wait_ge(s_x1[0], 4 * q + 4)
                    else:
                        pe.wait_ge(s_x1[1], 1)
                    if q >= 2:
                        pe.wait_ge(s_x1Tc[l], q - 1)
                    for i in range(4):
                        ins = t.transpose(bank[5 + q % 2][:, i * P:(i + 1) * P], x1[:, 4 * q + i, :], ident[:])
                    ins.then_inc(s_x1T[l], 1)

            def route_logits(l, w):
                pe.wait_ge(s_x1Tc[l], 4)
                for i in range(TT):
                    ins = t.matmul(Lp[:, i * E:(i + 1) * E], x1T[:, i, :], w, start=True, stop=True)
                ins.then_inc(s_lg[l], 1)

            def route_rank(l):
                pe.wait_ge(s_picked[l], 1)
                pe.wait_ge(s_const, 1)
                pk = picked[:].rearrange("p i e -> p (i e)")
                t.matmul(Rp, lower[:], pk, start=True, stop=False, skip_group_check=True)
                for i in range(TT):
                    n = TT - i
                    ins = t.matmul(Rp[:, (i + 1) * E:].rearrange("p (n e) -> p n e", e=E), ones[:],
                                   picked[:, i:i + 1, :].to_broadcast([P, n, E]), start=False, stop=(i == TT - 1),
                                   skip_group_check=True)
                ins.then_inc(s_rank[l], 1)

            def route_perm(l):
                n = TT * TOPK
                for c in range(n):
                    if c % 8 == 0:
                        pe.wait_ge(s_hot[l], c // 8 + 1)
                    ins = t.matmul(Mp, onehot[:, c, :], rhs[:, c, :], start=(c == 0), stop=(c == n - 1))
                ins.then_inc(s_perm[l], 1)

            def prepare1(e):
                pe.wait_ge(s_wl, e + 1)
                if e:
                    pe.wait_ge(s_mT, 2 * e)
                for c in range(CH):
                    ins = t.transpose(bank[0][:, c * P:(c + 1) * P], wraw[:, e, c * P:(c + 1) * P], ident[:])
                ins.then_inc(s_pT, 1)
                if e == 0:
                    pe.wait_ge(s_blk[0], 2)
                    pe.wait_ge(s_blk[1], 1)
                    pe.wait_ge(s_blk[2], 1)
                else:
                    pe.wait_ge(s_vT, e)
                pe.wait_ge(s_cig, e + 1)
                for c in range(CH):
                    o = c * (P + NH)
                    ins = t.matmul(bank[1][:, o:o + P + NH], blocks[:, 2 * r + e * CH + c, 0:P], cig[:, e % 2, c, :], start=True, stop=True)
                ins.then_inc(s_pV, 1)
                if e:
                    pe.wait_ge(s_kq, 2 * e)
                for c in range(CH):
                    o = c * (P + NH)
                    q, k = blocks[:, e * CH + c], blocks[:, r + e * CH + c]
                    t.matmul(bank[2][:, o:o + P + NH], k[:, 0:P], q, start=True, stop=False, skip_group_check=True)
                    ins = t.matmul(bank[2][:, o + P:o + P + NH], q[:, 0:P], igT[:, :, 6 * e + c], start=False, stop=True,
                                   skip_group_check=True)
                ins.then_inc(s_pKQ, 1)

            def prepare2(e):
                p = e % 2
                pe.wait_ge(s_mT, 2 * e + 2)
                if e:
                    pe.wait_ge(s_wc, e)
                for c in range(CH):
                    ins = t.transpose(bank[3][:, c * P:(c + 1) * P], mTs[:, p, c, :], ident[:])
                ins.then_inc(s_pWc, 1)
                pe.wait_ge(s_vT, e + 1)
                if e:
                    pe.wait_ge(s_rec, e)
                for c in range(CH):
                    ins = t.matmul(bank[4][:, c * P:(c + 1) * P + NH], mT[:, p, c, :], vT[:, p, c, :], start=(c == 0),
                                   stop=(c == CH - 1), skip_group_check=True)
                ins.then_inc(s_pWv, 1)

            route_transposes(0)
            pe.wait_ge(s_gate, 16)
            route_logits(0, gate[:])
            pe.wait_ge(s_parT, 1)
            prepare1(0)
            route_rank(0)
            for e in range(1, 5):
                prepare1(e)
                prepare2(e - 1)
            route_perm(0)
            for e in range(5, E):
                prepare1(e)
                prepare2(e - 1)
            prepare2(E - 1)
            pe.wait_ge(s_rec, E)
            pe.wait_ge(s_idx[0], 1)
            pe.wait_ge(s_late, 64)

            def in_transposes(l, u, b, dst):
                pe.wait_ge(s_gath[l][b], 32 * (u + 1))
                for h in range(HV):
                    ins = t.transpose(dst[:, h * P:(h + 1) * P], xg[:, b, h, :], ident[:])
                ins.then_inc(s_xtp[l], 1)

            def down(k, kb, l, dst):
                pe.wait_ge(s_wdbuf[l][kb], 16 * (k + 1))
                for h in range(HV):
                    for c in range(CH):
                        ins = t.matmul(dst[:, h * D:(h + 1) * D], hs[:, kb, c, h * P:(h + 1) * P],
                                       wdbuf[:, kb, c, :],
                                       start=(c == 0), stop=(c == CH - 1))
                ins.then_inc(s_y[l], 1)

            def step1(u, b):
                j = 2 * u + b
                up, k1, k2 = active(u, b), active(u, b, 1), active(u, b, 2)

                def project(dst, col, src, c):
                    return t.matmul(dst[:, c * TS:(c + 1) * TS], rbuf[:, b, col + c * P:col + (c + 1) * P], src,
                                    start=True, stop=True)

                if up:
                    pe.wait_ge(s_xts[0], j + 1)
                    pe.wait_ge(s_wbuf[0][b], 16 * (u + 1))
                    at_least(pe, s_pre, 2 * j)
                    for c in range(CH):
                        ins = project(PC, WC, xT[:, b, :], c)
                    ins.then_inc(s_pc, 1)
                    at_least(pe, s_vs, j - 1)
                    at_least(pe, s_stf, j)
                    for h in range(HV):
                        tok = slice(h * P, (h + 1) * P)
                        ins = t.matmul(VC[b][:, h * I:(h + 1) * I], xT[:, b, tok], rbuf[:, b, WV:WV + I], start=True, stop=True)
                        t.matmul(ig[:, h, :], xT[:, b, tok], rbuf[:, b, GX:GX + NH], start=(h == 0), stop=False,
                                 skip_group_check=True)
                    ins.then_inc(s_vc, 1)
                if k2:
                    k, kb = earlier(u, b, 2)
                    pe.wait_ge(s_hs, 2 * k + kb + 1)
                    at_least(pe, s_yb[0], 2 * k + kb)
                    down(k, kb, 0, Y)
                if up:
                    v, vb = earlier(u, b, -1)
                    if active(v, vb):
                        at_least(pe, s_h1, j - 1)
                        in_transposes(0, v, vb, XT)
                    at_least(pe, s_prod, j)
                    for c in range(CH):
                        pe.wait_ge(s_ca, CH * j + c + 1)
                        ins = project(A, KQ, ca[:, b, c, :], c)
                    ins.then_inc(s_a, 1)
                    for h in range(HV):
                        for c in range(CH):
                            t.matmul(ig[:, h, :], ca[:, b, c, h * P:(h + 1) * P], rbuf[:, b, GC + c * NH:GC + (c + 1) * NH],
                                     start=False, stop=(c == CH - 1), skip_group_check=True)
                    at_least(pe, s_zz, j)
                    for c in range(CH):
                        ins = project(Z, WZ, xT[:, b, :], c)
                    ins.then_inc(s_z, 1)
                if k1:
                    pe.wait_ge(s_vs, j)
                    if active(*earlier(u, b, -1)):
                        pe.wait_ge(s_xts[0], j + 2)
                    for c in range(CH):
                        for h in range(HV):
                            o = c * TS + h * P
                            ins = t.transpose(VT[:, o:o + P], vs[:, h, c * P:(c + 1) * P], ident[:])
                    ins.then_inc(s_vt, 1)
                if up:
                    pe.wait_ge(s_prod, j + 1)
                    for h in range(HV):
                        for c in range(CH):
                            ins = t.matmul(qk[:, h, :], prod[:, b, c, h * P:(h + 1) * P], headsum[:, c, :],
                                           start=False, stop=(c == CH - 1), skip_group_check=True)
                    ins.then_inc(s_st, 1)
            in_transposes(0, 0, 0, XT)
            steps(pe, step1, 2)

            route_transposes(1)
            route_logits(1, parT[:, 3 * r + E:3 * r + 2 * E])
            route_rank(1)
            route_perm(1)
            pe.wait_ge(s_idx[1], 1)

            def step2(u, b):
                j = 2 * u + b
                if active(u, b):
                    in_transposes(1, u, b, bank[b])
                    pe.wait_ge(s_xts[1], j + 1)
                    pe.wait_ge(s_wbuf[1][b], 16 * (u + 1))
                    at_least(pe, s_hh, j - 1)
                    for which, done in ((0, s_g), (1, s_u)):
                        for c in range(CH):
                            ins = t.matmul(bank[2 + 2 * which + b][:, c * TS:(c + 1) * TS],
                                           gubuf[:, b, which, c * P:(c + 1) * P], xT[:, b, :], start=True, stop=True)
                        ins.then_inc(done, 1)
                if active(u, b, 1):
                    k, kb = earlier(u, b, 1)
                    pe.wait_ge(s_hh, 2 * k + kb + 1)
                    at_least(pe, s_yb[1], 2 * k + kb - 1)
                    down(k, kb, 1, bank[6 + kb])
            steps(pe, step2, 1)

        @block.vector
        def _(dve):
            v = nc.vector
            count = [0]

            def done(ins):
                count[0] += 1
                ins.then_inc(s_dve, 1)
                dve.wait_ge(s_dve, count[0])

            def wide(ap, shape):
                return ap.to_broadcast(shape)

            def stats(src, cols):
                for i in cols:
                    ins = v.bn_stats(bn[:, i, :], src[:, i, :])
                done(ins)
                for i in cols:
                    ins = v.bn_aggr(mv[:, i, :], bn[:, i, :])
                return ins

            def route(l):
                dve.wait_ge(s_lg[l], 1)
                done(v.tensor_copy(lg[:], Lp.rearrange("p (i e) -> p i e", e=E)))
                row = [P, TT, E]
                for k in range(TOPK):
                    done(v.tensor_reduce(top[:, :, k], lg[:], AXX, ALU.max))
                    done(v.tensor_tensor(key[:], lg[:], wide(top[:, :, k:k + 1], row), ALU.is_equal))
                    done(v.tensor_tensor(key[:], key[:], wide(ekey[:].unsqueeze(1), row), ALU.mult))
                    done(v.tensor_reduce(kmax[:], key[:], AXX, ALU.max))
                    done(v.tensor_tensor(pick[:, :, k, :], key[:], wide(kmax[:].unsqueeze(2), row), ALU.is_equal))
                    if k == 0:
                        done(v.scalar_tensor_tensor(lg[:], pick[:, :, 0, :], -1e30, lg[:], ALU.mult, ALU.add))
                v.tensor_tensor(picked[:, 0:TT, :], pick[:, :, 0, :], pick[:, :, 1, :], ALU.add).then_inc(s_picked[l], 1)
                if l == 0:
                    v.tensor_tensor(den[:, :, 0], top[:, :, 1], top[:, :, 0], ALU.subtract).then_inc(s_top[0], 1)
                else:
                    v.tensor_scalar(den[:], top[:], -EXP_MAX, None, ALU.max).then_inc(s_top[1], 1)
                dve.wait_ge(s_rank[l], 1)
                sq8 = [P, E, E]
                done(v.tensor_tensor(cmp8[:], wide(Rp[:, TT * E:].unsqueeze(2), sq8), wide(tilecut[:].unsqueeze(1), sq8), ALU.is_gt))
                done(v.tensor_reduce(ntile[:], cmp8[:], AXX, ALU.add))
                done(v.tensor_tensor(cmp8[:], wide(ntile[:].unsqueeze(1), sq8), upto[:], ALU.mult))
                done(v.tensor_reduce(cum[:], cmp8[:], AXX, ALU.add))
                jrow = [1, NT + 1, E]
                done(v.tensor_tensor(cmpj[:], wide(cum[0:1, :].unsqueeze(1), jrow), wide(tileno[0:1, :].unsqueeze(2), jrow), ALU.is_le))
                done(v.tensor_reduce(ej[:], cmpj[:], AXX, ALU.add))
                v.tensor_scalar(expert[l][:], ej[:], float(E - 1), None, ALU.min).then_inc(s_exp[l], 1)
                done(v.tensor_tensor(before[:], cum[:], ntile[:], ALU.subtract))
                done(v.scalar_tensor_tensor(place[:], wide(before[:].unsqueeze(1), row), float(TS),
                                            Rp[:, 0:TT * E].rearrange("p (i e) -> p i e", e=E), ALU.mult, ALU.add))
                done(v.tensor_tensor(pslot[:], pick[:], wide(place[:].unsqueeze(2), [P, TT, TOPK, E]), ALU.mult))
                done(v.tensor_reduce(slot[:].rearrange("p (i k) -> p i k", k=TOPK), pslot[:], AXX, ALU.add))
                done(v.tensor_copy(sloti[:], slot[:]))
                v.tensor_scalar(loi[:], sloti[:], P - 1, None, ALU.bitwise_and)
                done(v.tensor_scalar(hii[:], sloti[:], 7, None, ALU.logical_shift_right))
                v.tensor_copy(lof[:], loi[:])
                done(v.tensor_copy(hif[:], hii[:]))
                n = TT * TOPK
                used = rhs[:, :, 2 * NA:3 * NA]
                done(v.tensor_tensor(used, wide(hif[:].unsqueeze(2), [P, n, NA]), wide(iota_a[:].unsqueeze(1), [P, n, NA]), ALU.is_equal))
                v.tensor_scalar(rhs[:, :, 0:NA], used, part[:, 0:1], None, ALU.mult)
                v.tensor_tensor(rhs[:, :, NA:2 * NA], used, wide(pairno[:].unsqueeze(2), [P, n, NA]), ALU.mult)
                for c in range(n):
                    ins = v.tensor_scalar(onehot[:, c, :], iota_p[:], lof[:, c:c + 1], None, ALU.is_equal)
                    if c % 8 == 7:
                        ins.then_inc(s_hot[l], 1)
                dve.wait_ge(s_ex[l], 1)
                if l == 0:
                    done(v.tensor_scalar(den[:, :, 1], ex[:, :, 0], 1.0, None, ALU.add))
                    done(v.reciprocal(wt[:, :, 0], den[:, :, 1]))
                    done(v.tensor_tensor(wt[:, :, 1], ex[:, :, 0], wt[:, :, 0], ALU.mult))
                    v.tensor_tensor(wsum[:], wt[:, :, 0], wt[:, :, 1], ALU.add)
                    done(v.tensor_scalar(wh[0][:], wt[:], 0.5, None, ALU.mult))
                else:
                    done(v.tensor_scalar(den[:], ex[:], 1.0, None, ALU.add))
                    done(v.reciprocal(wt[:], den[:]))
                    done(v.tensor_tensor(wsum[:], wt[:, :, 0], wt[:, :, 1], ALU.add))
                    done(v.tensor_scalar(wsum[:], wsum[:], 1e-10, None, ALU.add))
                    done(v.reciprocal(kmax[:], wsum[:]))
                    done(v.scalar_tensor_tensor(wh[1][:], wt[:], 0.5, wide(kmax[:].unsqueeze(2), [P, TT, TOPK]), ALU.mult, ALU.mult))
                dve.wait_ge(s_perm[l], 1)
                done(v.tensor_copy(perm[:], Mp))
                done(v.scalar_tensor_tensor(pairf[:], perm[:, 0:NA], float(TOPK * TT), perm[:, NA:2 * NA], ALU.mult, ALU.add))
                v.tensor_tensor(unused[:], perm[:, 2 * NA:3 * NA], spare[:], ALU.mult)
                done(v.tensor_copy(pairi[:], pairf[:]))
                v.tensor_scalar(gidx[l][:], pairi[:], 1, None, ALU.logical_shift_right)
                done(v.tensor_tensor(unused[:], spare[:], unused[:], ALU.subtract))
                v.tensor_tensor(sidx[l][:], pairf[:], unused[:], ALU.add).then_inc(s_idx[l], 1)

            dve.wait_ge(s_x, 32)
            done(stats(x, range(TT)))
            done(v.tensor_scalar(veps[:, 0, :], mv[:, :, 1], EPS, None, ALU.add))
            v.tensor_copy(kmax[:], veps[:, 0, :]).then_inc(s_veps[0], 1)
            v.scalar_tensor_tensor(veps[:, 1, :], veps[:, 0, :], EPS, mv[:, :, 1], ALU.mult, ALU.add).then_inc(s_veps[0], 1)
            dve.wait_ge(s_rstd[0], 1)
            for i in range(TT):
                v.tensor_scalar(x1[:, i, :], x[:, i, :], mv[:, i, 0:1], rstd[:, 0, i:i + 1], ALU.subtract, ALU.mult).then_inc(s_x1[0], 1)
            dve.wait_ge(s_rstd[0], 2)
            v.scalar_tensor_tensor(shift[:], mv[:, :, 0], -1.0, rstd[:, 1, :], ALU.mult, ALU.mult).then_inc(s_shift, 1)
            dve.wait_ge(s_parT, 1)
            for m in range(2):
                spread_blocks(v, m)
            dve.wait_ge(s_const, 1)
            route(0)
            for i in range(TT):
                ins = v.scalar_tensor_tensor(xres[:, i, :], x1[:, i, :], wsum[:, i:i + 1], x[:, i, :], ALU.mult, ALU.add)
            done(ins)

            K = 7

            def step1(u, b):
                j = 2 * u + b
                up, k1 = active(u, b), active(u, b, 1)
                kb = earlier(u, b, 1)[1]
                if k1:
                    dve.wait_ge(s_st, j)
                    base = K * (j - 1)
                    dve.wait_ge(s_onib, j)
                    v.scalar_tensor_tensor(nig0[:], ig, -1.0, onib[:, kb, CH:].unsqueeze(1).to_broadcast([P, HV, NH]),
                                           ALU.mult, ALU.subtract).then_inc(s_cell, 1)
                    v.tensor_copy(qks[:], qk).then_inc(s_stf, 1)
                    dve.wait_ge(s_cell, base + 1)
                    at_least(dve, s_eig, j - 1)
                    v.tensor_scalar(nig[:], nig0[:], EXP_MAX, None, ALU.min).then_inc(s_nig, 1)
                    dve.wait_ge(s_stf, j)
                    v.scalar_tensor_tensor(absqk[:], qks[:], -1.0, qks[:], ALU.mult, ALU.max).then_inc(s_cell, 1)
                    dve.wait_ge(s_cell, base + 2)
                    v.tensor_scalar(abs6[:], absqk[:], CELL_EPS, None, ALU.add).then_inc(s_cell, 1)
                    dve.wait_ge(s_cell, base + 3)
                    dve.wait_ge(s_eig, j)
                    v.scalar_tensor_tensor(nrm6[:], eig[:], CELL_EPS, abs6[:], ALU.add, ALU.max).then_inc(s_cell, 1)
                    dve.wait_ge(s_cell, base + 4)
                    v.reciprocal(rn[:], nrm6[:]).then_inc(s_cell, 1)
                    dve.wait_ge(s_cell, base + 5)
                    v.tensor_tensor(cc[:], qks[:], rn[:], ALU.mult).then_inc(s_cell, 1)
                    dve.wait_ge(s_cell, base + 6)
                    v.tensor_tensor(c2[:], cc[:], cc[:], ALU.mult).then_inc(s_cell, 1)
                    dve.wait_ge(s_cell, base + 7)
                    dve.wait_ge(s_var, j)
                    v.tensor_tensor(c2v[:], var[:, kb], c2[:], ALU.mult).then_inc(s_c2v, 1)
                    dve.wait_ge(s_c2v, j)
                    at_least(dve, s_rh, j - 1)
                    v.tensor_scalar(c2ve[:], c2v[:], EPS, None, ALU.add).then_inc(s_c2ve, 1)
                if up:
                    dve.wait_ge(s_thc, j + 1)
                    at_least(dve, s_st, j - 1)
                    at_least(dve, s_cask, j - 1)
                    for c in range(CH):
                        v.scalar_tensor_tensor(ca[:, b, c], thc[:, b, c], 1.0, pre[:, b, c], ALU.add, ALU.mult).then_inc(s_ca, 1)
                if k1:
                    dve.wait_ge(s_thz, j)
                    v.scalar_tensor_tensor(zz[:, kb], thz[:, kb], 1.0, Z[:].rearrange("p (c t) -> p c t", c=CH), ALU.add, ALU.mult).then_inc(s_zz, 1)
                    dve.wait_ge(s_rh, j)
                    v.tensor_tensor(ss[:].rearrange("p (h k) -> p h k", h=HV), cc[:], rh[:], ALU.mult).then_inc(s_ss, 1)
                    dve.wait_ge(s_ss, j)
                    at_least(dve, s_vt, j - 1)
                    v.tensor_tensor(vs[:].rearrange("p h (k d) -> p (h k) d", d=DH), VC[kb][:].rearrange("p (k d) -> p k d", d=DH),
                                    ss[:].unsqueeze(2).to_broadcast([P, HV * NH, DH]), ALU.mult).then_inc(s_vs, 1)
                if up:
                    dve.wait_ge(s_a, j + 1)
                    v.tensor_tensor(prod[:, b], A[:].rearrange("p (c t) -> p c t", c=CH), ca[:, b], ALU.mult).then_inc(s_prod, 1)
                    dve.wait_ge(s_wbuf[0][b], 16 * (u + 1))
                    v.tensor_copy(onib[:, b], rbuf[:, b, ON:ON + CH + NH]).then_inc(s_onib, 1)
                if k1:
                    dve.wait_ge(s_vt, j)
                    dve.wait_ge(s_cask, j)
                    for c in range(CH):
                        ins = v.scalar_tensor_tensor(h1[:, c, :], VT[:, c * TS:(c + 1) * TS], onib[:, kb, c:c + 1],
                                                     cask[:, kb, c, :], ALU.mult, ALU.add)
                    ins.then_inc(s_h1, 1)
                    dve.wait_ge(s_h1, j)
                    at_least(dve, s_y[0], j - 2)
                    v.tensor_tensor(hs[:, kb], h1[:], zz[:, kb], ALU.mult).then_inc(s_hs, 1)
            steps(dve, step1, 1)

            def combine(l, c):
                cols = range(c * TT // 4, (c + 1) * TT // 4)
                dve.wait_ge(s_yin[l][c], 16)
                for k in range(TOPK):
                    for i in cols:
                        ins = v.scalar_tensor_tensor(xres[:, i, :], ypair[:, TOPK * i + k, :], wh[l][:, i, k:k + 1], xres[:, i, :], ALU.mult, ALU.add)
                    if k == 0:
                        done(ins)
                return ins, cols

            for c in range(4):
                ins, cols = combine(0, c)
                done(ins)
                ins = stats(xres, cols)
            done(ins)
            v.tensor_scalar(veps[:, 0, :], mv[:, :, 1], EPS, None, ALU.add).then_inc(s_veps[1], 1)
            dve.wait_ge(s_rstd[1], 1)
            for i in range(TT):
                ins = v.tensor_scalar(x1[:, i, :], xres[:, i, :], mv[:, i, 0:1], rstd[:, 0, i:i + 1], ALU.subtract, ALU.mult)
            ins.then_inc(s_x1[1], 1)
            route(1)

            def step2(u, b):
                if not active(u, b):
                    return
                j = 2 * u + b
                dve.wait_ge(s_thg, j + 1)
                v.scalar_tensor_tensor(ca[:, b], thc[:, b], 1.0, bank[2 + b][:].rearrange("p (c t) -> p c t", c=CH), ALU.add, ALU.mult).then_inc(s_gg, 1)
                dve.wait_ge(s_gg, j + 1)
                dve.wait_ge(s_u, j + 1)
                at_least(dve, s_y[1], j - 1)
                v.tensor_tensor(hs[:, b], bank[4 + b][:].rearrange("p (c t) -> p c t", c=CH), ca[:, b], ALU.mult).then_inc(s_hh, 1)
            steps(dve, step2, 0)
            for c in range(4):
                combine(1, c)[0].then_inc(s_out, 1)


_INS = ["hidden_states", "gate_w", "ln_w", "w_up", "conv_w", "conv_b", "q_w", "k_w", "v_w", "ig_w", "ig_b",
        "on_w", "skip_w", "w_down"]
_FFN = ["router_w", "w_gate", "w_up", "w_down"]


def kernel(**inputs):
    import numpy as _np
    import concourse.bacc as _bacc
    from concourse import mybir as _mybir
    from concourse.bass_utils import run_bass_kernel_spmd as _run

    nc = _bacc.Bacc("TRN2", target_bir_lowering=False, num_devices=1)
    arrays, args = {}, []
    for name in ["L0_attn_" + n for n in _INS] + ["L0_ffn_" + n for n in _FFN]:
        a = _np.ascontiguousarray(inputs[name])
        arrays[f"in_{name}"] = a
        args.append(nc.dram_tensor(f"in_{name}", a.shape, _mybir.dt.from_np(a.dtype), kind="ExternalInput").ap())
    args.append(nc.dram_tensor("out_0", inputs["L0_attn_hidden_states"].shape, _mybir.dt.float32, kind="ExternalOutput").ap())
    program(nc, *args)
    return _run(nc, [arrays], core_ids=[0]).results[0]["out_0"]
```

```python
from contextlib import ExitStack

import concourse.bass as bass
from concourse import mybir

ALU = mybir.AluOpType
ACT = mybir.ActivationFunctionType
F32 = mybir.dt.float32
BF16 = mybir.dt.bfloat16
I32 = mybir.dt.int32
U32 = mybir.dt.uint32
AXX = mybir.AxisListType.X

P = 128
NTOK, D = 2048, 128
TT = NTOK // P
E, TOPK = 8, 2
I = 256
CH = I // P
NH, QB = 4, 4
DH = I // NH
NB = P // QB
TS = 256
HV = TS // P
NT = (TOPK * NTOK + E * (TS - 1)) // TS
NA = NT * HV
LTS = (TS, P)
LNT = (NT, (TOPK * NTOK + E * (P - 1)) // P)
WAYS = (2, 4)
PAIRS = TOPK * NTOK
EPS = 1e-5
CELL_EPS = 1e-6
EXP_MAX = 85.0
assert LNT[1] <= NA <= P and P * 2 * TT == PAIRS

WC, WZ, KQ, WV = 0, I, 2 * I, 3 * I
GX, GC = 4 * I, 4 * I + NH
CB, SK, ON = GC + CH * NH, GC + CH * NH + CH, GC + CH * NH + 2 * CH
IB = ON + CH
REC = IB + NH

GATE, UP, DOWN, REC2 = 0, I, 2 * I, 2 * I + CH * D


def at_least(eng, sem, value):
    if not isinstance(value, int) or value > 0:
        eng.wait_ge(sem, value)


def program(nc, hidden, gate_w, ln_w, w_up, conv_w, conv_b, q_w, k_w, v_w, ig_w, ig_b, on_w,
            skip_w, w_down, router_w, f_gate, f_up, f_down, out):
    with ExitStack() as ctx:
        def sb(name, shape, dt=F32):
            return ctx.enter_context(nc.sbuf_tensor(name, shape, dt))

        def sem(name):
            return ctx.enter_context(nc.semaphore(name))

        bank = [ctx.enter_context(nc.psum_tensor(f"bank{i}", [P, 512], F32)) for i in range(8)]

        xrows = [nc.dram_tensor(f"xrows{l}", [NTOK, D], F32, kind="Internal").ap() for l in range(2)]
        yrows = [nc.dram_tensor(f"yrows{l}", [PAIRS + NT * TS, D], F32, kind="Internal").ap() for l in range(2)]

        ident = sb("ident", [P, P])
        lower = sb("lower", [P, P], BF16)
        ones = sb("ones", [P, P], BF16)
        iota_p = sb("iota_p", [P, P], BF16)
        iota_a = sb("iota_a", [P, NA])
        part = sb("part", [P, 1])
        pairno = sb("pairno", [P, TT * TOPK])
        spare = sb("spare", [P, NA])
        ekey = sb("ekey", [P, E])
        tilecut = sb("tilecut", [P, NTOK // P])
        upto = sb("upto", [P, E, E])
        tileno = sb("tileno", [P, LNT[1] + 1])
        blockmask = sb("blockmask", [P, NB])
        headmask = sb("headmask", [P, 2])
        centre = sb("centre", [P, P])
        headsum = sb("headsum", [P, CH, NH])
        neghalf = sb("neghalf", [P, TT])

        x = sb("x", [P, TT, D])
        x1 = sb("x1", [P, TT, D])
        xn = sb("xn", [P, TT, D])
        xres = x
        x1T = sb("x1T", [P, TT, P])
        bn = sb("bn", [P, TT, 6])
        mv = sb("mv", [P, TT, 2])
        veps = sb("veps", [P, 2, TT])
        rstd = sb("rstd", [P, 2, TT])
        nmean = sb("nmean", [P, TT])
        shift = sb("shift", [P, 2, TT])

        lg = sb("lg", [P, TT, E])
        key = sb("key", [P, TT, E])
        top = sb("top", [P, TT, TOPK])
        kmax = sb("kmax", [P, TT])
        pick = sb("pick", [P, TT, TOPK, E])
        picked = sb("picked", [P, TT + 1, E], BF16)
        cmpn = sb("cmpn", [P, E, NTOK // P])
        cmp8 = sb("cmp8", [P, E, E])
        ntile = sb("ntile", [P, E])
        cum = sb("cum", [P, E])
        before = sb("before", [P, E])
        place = sb("place", [P, TT, E])
        pslot = sb("pslot", [P, TT, TOPK, E])
        slot = sb("slot", [P, TT * TOPK])
        sloti = sb("sloti", [P, TT * TOPK], I32)
        loi = sb("loi", [P, TT * TOPK], I32)
        hii = sb("hii", [P, TT * TOPK], I32)
        lof = sb("lof", [P, TT * TOPK])
        hif = sb("hif", [P, TT * TOPK])
        cmpj = sb("cmpj", [1, LNT[1] + 1, E])
        ej = sb("ej", [1, LNT[1] + 1])
        expert = [sb(f"expert{l}", [1, LNT[l] + 1], I32) for l in range(2)]
        onehot = sb("onehot", [P, TT * TOPK, P], BF16)
        rhs = sb("rhs", [P, TT * TOPK, 3 * NA], BF16)
        perm = sb("perm", [P, 3 * NA])
        pairf = sb("pairf", [P, NA])
        unused = sb("unused", [P, NA])
        pairi = sb("pairi", [P, NA], U32)
        gidx = [sb(f"gidx{l}", [P, NA], U32) for l in range(2)]
        sidx = [sb(f"sidx{l}", [P, NA], U32) for l in range(2)]
        ex = sb("ex", [P, TT, TOPK])
        den = sb("den", [P, TT, TOPK])
        wt = sb("wt", [P, TT, TOPK])
        wsum = sb("wsum", [P, TT])
        wh = [sb(f"wh{l}", [P, TT, TOPK]) for l in range(2)]

        vs = sb("vs", [P, HV, I])
        h1 = sb("h1", [P, CH, TS])
        raw1 = vs[:].rearrange("p h n -> p (h n)")[0:64, :]
        raw2 = h1[:].rearrange("p c t -> p (c t)")[0:48, :]
        raw3 = sb("raw3", [64, P])
        gate = sb("gate", [P, E])
        qkvT = sb("qkvT", [P, QB, 64])
        igT = sb("igT", [P, NH, 48])
        parT = sb("parT", [P, 64])
        wraw = sb("wraw", [P, E, 2 * I])
        blocks = sb("blocks", [P, 3 * E * CH, P + NH])
        cig = sb("cig", [P, 2, CH, P + NH])
        mT = sb("mT", [P, 2, CH, P])
        mTs = sb("mTs", [P, 2, CH, P])
        vT = sb("vT", [P, 2, CH, P + NH])
        rec = sb("rec", [P, E, REC])
        wd1 = sb("wd1", [P, E, CH, D])
        rec2 = sb("rec2", [P, E, REC2])
        ypair = blocks[:, 0:2 * E * CH, 0:D]

        gi = sb("gi", [P, 2, HV], U32)
        si = sb("si", [P, 2, HV], U32)
        wbuf = sb("wbuf", [P, max(2 * (REC + CH * D), WAYS[1] * REC2)])
        rbuf = wbuf[:, 0:2 * REC].rearrange("p (b n) -> p b n", b=2)
        wdbuf = wbuf[:, 2 * REC:2 * (REC + CH * D)].rearrange("p (b c d) -> p b c d", b=2, c=CH)
        r2buf = wbuf[:, 0:WAYS[1] * REC2].rearrange("p (b n) -> p b n", b=WAYS[1])
        xg = sb("xg", [P, 2, HV, D])
        xT = sb("xT", [P, 2, TS])
        pre = sb("pre", [P, 2, CH, TS])
        def tiles(buf, n):
            return buf[:].rearrange("p a b -> p (a b)")[:, n * 2 * I * 2:(n + 1) * 2 * I * 2]\
                .rearrange("p (b c t) -> p b c t", b=2, c=CH)

        thc, thz = tiles(xn, 0), tiles(xn, 1)
        sq, hs = tiles(x1T, 0)[:, 0], tiles(x1T, 1)
        ca, zz, cask, prod = (tiles(wraw, n) for n in range(4))

        def halved(t):
            return t.rearrange("p b c t -> p (b c t)").rearrange("p (b c t) -> p b c t", b=WAYS[1], c=CH)

        th2, gg2, hh2 = halved(thc), halved(ca), halved(hs)
        onib = sb("onib", [P, 2, CH + NH])
        yb = sb("yb", [P, 2, HV, D])
        xg2, yb2 = (t[:].rearrange("p b h d -> p (b h) d") for t in (xg, yb))
        gi2, si2 = (t[:].rearrange("p b h -> p (b h)") for t in (gi, si))
        xT2 = xT[:].rearrange("p b (h t) -> p (b h) t", h=HV)
        nig0 = sb("nig0", [P, HV, NH])
        nig = sb("nig", [P, HV, NH])
        eig = sb("eig", [P, HV, NH])
        qks = sb("qks", [P, HV, NH])
        absqk = sb("absqk", [P, HV, NH])
        nrm6 = sb("nrm6", [P, HV, NH])
        abs6 = sb("abs6", [P, HV, NH])
        rn = sb("rn", [P, HV, NH])
        cc = sb("cc", [P, HV, NH])
        c2 = sb("c2", [P, HV, NH])
        var = sb("var", [P, 2, HV, NH])
        c2v = sb("c2v", [P, HV, NH])
        c2ve = sb("c2ve", [P, HV, NH])
        rh = sb("rh", [P, HV, NH])
        ss = sb("ss", [P, HV * NH])

        s_x = [sem(f"x_loaded{c}") for c in range(4)]
        s_raw, s_gate, s_wraw, s_ib, s_late = (sem(n) for n in (
            "raw_loaded", "gate_loaded", "wup_loaded", "igb_loaded", "late_loaded"))
        s_pool = sem("pool_step")
        s_const = sem("consts_ready")
        s_dve = sem("dve_step")
        s_veps = [sem(f"veps_ready{l}") for l in range(2)]
        s_rstd = [sem(f"rstd_ready{l}") for l in range(2)]
        s_x1 = [sem(f"normed_ready{l}") for l in range(2)]
        s_xn = sem("xn_ready")
        s_used, s_paired = sem("used_ready"), sem("paired_ready")
        s_vepsn = sem("veps_xn_ready")
        s_rstdn = sem("rstd_xn_ready")
        s_x1T = [sem(f"normedT_psum{l}") for l in range(2)]
        s_x1Tc = [sem(f"normedT_copied{l}") for l in range(2)]
        s_lg = [sem(f"logits_ready{l}") for l in range(2)]
        s_top = [sem(f"top_ready{l}") for l in range(2)]
        s_ex = [sem(f"topexp_ready{l}") for l in range(2)]
        s_picked = [sem(f"picked_ready{l}") for l in range(2)]
        s_rank = [sem(f"rank_ready{l}") for l in range(2)]
        s_hot = [sem(f"onehots_ready{l}") for l in range(2)]
        s_perm = [sem(f"perm_ready{l}") for l in range(2)]
        s_idx = [sem(f"indices_ready{l}") for l in range(2)]
        s_exp = [sem(f"experts_ready{l}") for l in range(2)]
        s_rows = [sem(f"xrows_stored{l}") for l in range(2)]
        s_parp, s_parT, s_wl = sem("par_psum"), sem("par_copied"), sem("wl_ready")
        s_blk = [sem(f"blocks_ready{m}") for m in "qkv"]
        s_wz = sem("wz_ready")
        s_cig = sem("cig_ready")
        s_pT, s_pV, s_pKQ, s_pWc, s_pWv = (sem(n) for n in ("mT_psum", "vT_psum", "kq_psum", "wc_psum", "wv_psum"))
        s_mT, s_vT, s_kq, s_wc, s_rec = (sem(n) for n in ("mT_copied", "vT_copied", "kq_copied", "wc_copied", "record_ready"))
        s_par2 = sem("params_in_record")
        s_gath = [[sem(f"gathered{l}{b}") for b in range(WAYS[l])] for l in range(2)]
        s_scat = [[sem(f"scattered{l}{b}") for b in range(WAYS[l])] for l in range(2)]
        s_wbuf = [[sem(f"weights_in{l}{b}") for b in range(WAYS[l])] for l in range(2)]
        s_wdbuf = [sem(f"wdown_in{b}") for b in range(2)]
        s_gi = [sem(f"gi_copied{l}") for l in range(2)]
        s_issue = sem("pool_issues")
        s_si = [sem(f"si_copied{l}") for l in range(2)]
        s_xtp = [sem(f"xT_psum{l}") for l in range(2)]
        s_xts = [sem(f"xT_copied{l}") for l in range(2)]
        s_y = [sem(f"y_psum{l}") for l in range(2)]
        s_yb = [sem(f"y_copied{l}") for l in range(2)]
        s_pc, s_vc, s_z, s_a, s_ig, s_st, s_vt = (sem(n) for n in (
            "conv_psum", "v_psum", "z_psum", "kqca_psum", "ig_psum", "stats_psum", "vT_tile_psum"))
        s_pre, s_thc, s_cask, s_thz, s_eig = (sem(n) for n in (
            "pre_ready", "tanh_conv", "skip_ready", "tanh_z", "exp_ig"))
        s_nig, s_cell, s_stf, s_var, s_c2v, s_c2ve, s_rh, s_ss = (sem(n) for n in (
            "nig_ready", "cell_step", "stats_read", "var_ready", "c2v_ready", "c2ve_ready", "rstd_h", "scale_ready"))
        s_onib, s_ca, s_prod, s_zz, s_vs, s_h1, s_hs = (sem(n) for n in (
            "onib_copied", "ca_ready", "prod_ready", "zz_ready", "vs_ready", "h1_ready", "hs_ready"))
        s_g, s_thg, s_gg, s_hh = (sem(n) for n in ("gate_up_psum", "tanh_gate", "gated", "ffn_h"))
        s_yin = [[sem(f"ypair_loaded{l}{c}") for c in range(4)] for l in range(2)]
        s_out = sem("out_ready")
        s_st_out = sem("out_stored")

        out_v = out.rearrange("b s d -> (b s) d").rearrange("(p i) d -> p i d", i=TT)
        x_v = hidden.rearrange("b s d -> (b s) d").rearrange("(p i) d -> p i d", i=TT)
        Lp, Rp, Mp = bank[7][:, 0:TT * E], bank[7][:, 128:128 + (TT + 1) * E], bank[7][:, 288:288 + 3 * NA][:, 0:138]
        Mp = bank[5][:, 0:3 * NA]
        XT, PC, VC, Z, A, ST, Y = bank[0], bank[1], bank[2:4], bank[4], bank[5], bank[6], bank[7]
        VT = XT
        qk = ST[:, 0:HV * 8].rearrange("p (h k) -> p h k", h=HV)[:, :, 0:4]
        ig = ST[:, 0:HV * 8].rearrange("p (h k) -> p h k", h=HV)[:, :, 4:8]

        block = ctx.enter_context(nc.Block())

        def steps(eng, step, l, lag, head=1):
            w, n = WAYS[l], LNT[l]
            full = (n - w) // w
            for j in range(head * w):
                step(j // w, j % w)
            with eng.Fori(head, full) as u:
                for b in range(w):
                    step(u, b)
            for j in range(full * w, n + lag):
                step(j // w, j % w)

        def active(l, u, b, back=0):
            return not isinstance(u, int) or 0 <= WAYS[l] * u + b - back < LNT[l]

        def earlier(l, u, b, back):
            w = WAYS[l]
            return (u - (back - b + w - 1) // w, (b - back) % w)

        def quarter(c):
            return slice(c * TT // 4, (c + 1) * TT // 4)

        @block.sync
        def _(sp):
            for c in range(4):
                sp.dma_start(x[:, quarter(c), :], x_v[:, quarter(c), :]).then_inc(s_x[c], 16)
            sp.dma_start(gate[:], gate_w).then_inc(s_gate, 16)
            r = E * CH
            for m, w in enumerate((conv_b, on_w, skip_w)):
                sp.dma_start(raw3[m * r:(m + 1) * r, :], w.rearrange("e (c p) -> (e c) p", c=CH)).then_inc(s_raw, 16)
            sp.dma_start(raw3[3 * r:3 * r + E, :], ln_w).then_inc(s_raw, 16)
            sp.dma_start(raw3[3 * r + E:3 * r + 2 * E, :], router_w).then_inc(s_raw, 16)
            sp.dma_start(rec[:, :, IB:IB + NH], ig_b.unsqueeze(0).to_broadcast([P, E, NH])).then_inc(s_ib, 16)
            sp.dma_start(wraw[:], w_up.rearrange("e d n -> d e n")).then_inc(s_wraw, 16)
            sp.wait_ge(s_raw, 16 * 10)
            sp.dma_start(wd1[:], w_down.rearrange("e (c p) d -> p e c d", p=P)).then_inc(s_late, 16)
            sp.dma_start(rec2[:, :, GATE:GATE + I], f_gate.rearrange("e d n -> d e n")).then_inc(s_late, 16)
            sp.dma_start(rec2[:, :, UP:UP + I], f_up.rearrange("e d n -> d e n")).then_inc(s_late, 16)
            for c in range(CH):
                sp.dma_start(rec2[:, :, DOWN + c * D:DOWN + (c + 1) * D],
                             f_down.rearrange("e (c p) d -> p e c d", p=P)[:, :, c, :]).then_inc(s_late, 16)

            sp.wait_ge(s_xn, 2)
            sp.dma_start(xrows[0].rearrange("(p i) d -> p i d", i=TT), xn[:]).then_inc(s_rows[0], 16)

            sp.wait_ge(s_exp[0], 1)
            sp.wait_ge(s_rec, E)
            sp.wait_ge(s_par2, 3)
            sp.wait_ge(s_kq, 2 * E)
            sp.wait_ge(s_wc, E)
            sp.wait_ge(s_wz, E)
            sp.wait_ge(s_late, 80)

            def load_expert(l, u, b, body):
                if active(l, u, b):
                    body(sp.value_load(expert[l][0:1, bass.ds(WAYS[l] * u + b, 1)], min_val=0, max_val=E - 1))

            def load_down(u, b):
                def body(e):
                    at_least(sp, s_y[0], 2 * u + b - 1)
                    sp.dma_start(wdbuf[:, b], wd1[:, bass.ds(e, 1), :, :].rearrange("p a c d -> p (a c) d"))\
                        .then_inc(s_wdbuf[b], 16)
                load_expert(0, u, b, body)

            def load1(u, b):
                def body(e):
                    j = 2 * u + b
                    at_least(sp, s_ig, j - 1)
                    at_least(sp, s_cask, j - 1)
                    at_least(sp, s_onib, j - 1)
                    sp.dma_start(rbuf[:, b, :], rec[:, bass.ds(e, 1), :].rearrange("p a n -> p (a n)"))\
                        .then_inc(s_wbuf[0][b], 16)
                load_expert(0, u, b, body)
                load_down(*earlier(0, u, b, 2))
            steps(sp, load1, 0, 2, head=2)

            def load_pairs(l):
                for b in range(WAYS[l]):
                    sp.wait_ge(s_scat[l][b], 16 * (LTS[l] // P) * ((LNT[l] - b + WAYS[l] - 1) // WAYS[l]))
                yv = yrows[l][0:PAIRS, :].rearrange("(p m) d -> p m d", p=P)
                for c in range(4):
                    m = PAIRS // P // 4
                    sp.dma_start(ypair[:, c * m:(c + 1) * m, :], yv[:, c * m:(c + 1) * m, :])\
                        .then_inc(s_yin[l][c], 16)
            load_pairs(0)

            sp.wait_ge(s_x1[1], 4)
            sp.dma_start(xrows[1].rearrange("(p i) d -> p i d", i=TT), x1[:]).then_inc(s_rows[1], 16)
            sp.wait_ge(s_exp[1], 1)
            sp.wait_ge(s_late, 80)

            def load2(u, b):
                def body(e):
                    at_least(sp, s_y[1], 4 * u + b - 3)
                    sp.dma_start(r2buf[:, b, :], rec2[:, bass.ds(e, 1), :].rearrange("p a n -> p (a n)"))\
                        .then_inc(s_wbuf[1][b], 16)
                load_expert(1, u, b, body)
            steps(sp, load2, 1, 0)
            load_pairs(1)
            for c in range(4):
                m = TT // 4
                sp.wait_ge(s_out, c + 1)
                sp.dma_start(out_v[:, c * m:(c + 1) * m, :], xres[:, c * m:(c + 1) * m, :])\
                    .then_inc(s_st_out, 16)
            sp.wait_ge(s_st_out, 64)

        def paired(eng):
            n = TT * TOPK
            eng.tensor_tensor(rhs[:, :, NA:2 * NA], rhs[:, :, 2 * NA:], pairno[:].unsqueeze(2).to_broadcast([P, n, NA]), ALU.mult)\
                .then_inc(s_paired, 1)

        def spread_blocks(m):
            n = E * CH
            nc.vector.tensor_tensor(
                blocks[:, m * n:(m + 1) * n, 0:P].rearrange("p m (n b) -> p m n b", b=QB),
                blockmask[:][:, None, :, None].to_broadcast([P, n, NB, QB]),
                qkvT[:, :, m * n:(m + 1) * n].rearrange("p b m -> p m b").unsqueeze(2).to_broadcast([P, n, NB, QB]),
                ALU.mult).then_inc(s_blk[m], 1)
            if m == 0:
                nc.vector.tensor_copy(blocks[:, 0:n, P:].rearrange("p (e c) h -> p e c h", c=CH),
                                igT[:].rearrange("p h (e s) -> p e s h", e=E)[:, :, CH:2 * CH, :]).then_inc(s_blk[m], 1)

        @block.gpsimd
        def _(pool):
            g = nc.gpsimd
            count = [0]

            def done(ins):
                count[0] += 1
                ins.then_inc(s_pool, 1)
                pool.wait_ge(s_pool, count[0])

            def select(t, pattern, base, cm, op=ALU.is_ge):
                done(g.affine_select(out=t, in_=t, compare_op=op, fill=0.0, base=base,
                                     pattern=pattern, channel_multiplier=cm))

            done(g.memset(ident[:], 0.0))
            done(g.affine_select(out=ident[:], in_=ident[:], compare_op=ALU.not_equal, fill=1.0, base=0,
                                 pattern=[[-1, P]], channel_multiplier=1))
            g.memset(picked[:], 0.0)
            g.memset(neghalf[:], -0.5)
            done(g.memset(blockmask[:], 1.0))
            select(blockmask[:], [[-QB, NB]], 0, 1)
            select(blockmask[:], [[QB, NB]], QB - 1, -1)
            def norms(k, cols, sem_out):
                done(g.tensor_tensor(rstd[:, k, cols], veps[:, k, cols], neghalf[:, cols], ALU.pow))
                g.tensor_tensor(shift[:, k, cols], nmean[:, cols], rstd[:, k, cols], ALU.mult).then_inc(sem_out, 1)

            for c in range(4):
                pool.wait_ge(s_veps[0], c + 1)
                norms(0, quarter(c), s_rstd[0])
            done(g.memset(headmask[:], 1.0))
            select(headmask[:], [[-DH, 2]], 0, 1)
            select(headmask[:], [[DH, 2]], DH - 1, -1)
            done(g.memset(headsum[:], 0.0))
            for c in range(CH):
                g.tensor_scalar(headsum[:, c, 2 * c:2 * c + 2], headmask[:], DH ** -0.5 / 4, None, ALU.mult)
            done(g.tensor_scalar(centre[:].rearrange("p (k r) -> p k r", k=2),
                                 headmask[:].unsqueeze(2).to_broadcast([P, 2, DH]), -1.0 / DH, None, ALU.mult))
            done(g.tensor_tensor(centre[:], centre[:], ident[:], ALU.add))
            for p in range(2):
                g.tensor_copy(cig[:, p, 0, 0:P], centre[:])
                g.tensor_copy(cig[:, p, 1, NH:], centre[:])
            small = dict(allow_small_or_imprecise_dtypes=True)
            done(g.iota(ekey[:], pattern=[[-1, E]], base=E, channel_multiplier=0, **small))
            done(g.memset(lower[:], 1.0))
            select(lower[:], [[1, P]], -1, -1)
            g.memset(ones[:], 1.0)
            done(g.memset(upto[:], 1.0))
            select(upto[:], [[1, E], [-1, E]], 0, 0)
            g.iota(tilecut[:], pattern=[[P, NTOK // P]], base=0, channel_multiplier=0, **small)
            g.iota(tileno[:], pattern=[[1, LNT[1] + 1]], base=0, channel_multiplier=0, **small)
            g.iota(iota_p[:], pattern=[[1, P]], base=0, channel_multiplier=0, **small)
            g.iota(iota_a[:], pattern=[[1, NA]], base=0, channel_multiplier=0, **small)
            g.iota(part[:], pattern=[[0, 1]], base=0, channel_multiplier=1, **small)
            g.iota(pairno[:], pattern=[[1, TT * TOPK]], base=0, channel_multiplier=0, **small)
            done(g.iota(spare[:], pattern=[[P, NA]], base=PAIRS, channel_multiplier=1, **small))
            g.memset(cmpj[:], 0.0).then_inc(s_const, 1)

            pool.wait_ge(s_parT, 1)
            pool.wait_ge(s_wraw, 16)
            at = 3 * E * CH

            def fold(e):
                w = parT[:, at + e:at + e + 1]
                g.tensor_scalar(wraw[:, e, 0:I], wraw[:, e, 0:I], w, None, ALU.mult).then_inc(s_wl, 1)
                if e >= 2:
                    pool.wait_ge(s_pV, e - 1)
                g.tensor_copy(cig[:, e % 2].rearrange("p c n -> p (c n)")[:, P:P + CH * NH].rearrange("p (c h) -> p c h", c=CH),
                              igT[:, :, 6 * e + 2 * CH:6 * e + 3 * CH].rearrange("p h c -> p c h")).then_inc(s_cig, 1)

            for e in range(2):
                fold(e)
            pool.wait_ge(s_vepsn, 1)
            norms(1, slice(0, TT), s_rstdn)
            pool.wait_ge(s_rstdn, 1)

            def renormed(i):
                return g.tensor_scalar(xn[:, i, :], x[:, i, :], rstd[:, 1, i:i + 1], shift[:, 1, i:i + 1], ALU.mult, ALU.add)

            for e in range(2, E):
                fold(e)
                renormed(e - 2)
            for i in range(E - 2, TT // 2):
                ins = renormed(i)
            ins.then_inc(s_xn, 1)

            def columns(l, b):
                if l:
                    return [(xg2[:, b, :], yb2[:, b, :], gi2[:, b:b + 1], si2[:, b:b + 1])]
                return [(xg[:, b, h, :], yb[:, b, h, :], gi[:, b, h:h + 1], si[:, b, h:h + 1]) for h in range(HV)]

            def gather(l, u, b):
                if not active(l, u, b):
                    return
                j = WAYS[l] * u + b
                at_least(pool, s_xtp[l], j - WAYS[l] + 1)
                pool.wait_ge(s_rows[l], 16)
                pool.wait_ge(s_gi[l], j + 1)
                pool.sem_inc(s_issue, 1)
                for rows, _, index, _ in columns(l, b):
                    g.indirect_dma_start(
                        rows, None, xrows[l], bass.IndirectOffsetOnAxis(ap=index, axis=0)).then_inc(s_gath[l][b], 16)

            def scatter(l, u, b):
                if not active(l, u, b):
                    return
                j = WAYS[l] * u + b
                pool.wait_ge(s_si[l], j + 1)
                pool.wait_ge(s_yb[l], j + 1)
                pool.sem_inc(s_issue, 1)
                for _, rows, _, index in columns(l, b):
                    g.indirect_dma_start(
                        yrows[l], bass.IndirectOffsetOnAxis(ap=index, axis=0), rows, None).then_inc(s_scat[l][b], 16)

            for b in range(2):
                gather(0, 0, b)

            def step1(u, b):
                k, kb = earlier(0, u, b, 1)
                if active(0, k, kb):
                    pool.wait_ge(s_c2ve, 2 * k + kb + 1)
                    at_least(pool, s_ss, 2 * k + kb)
                    g.tensor_tensor(rh[:], c2ve[:], neghalf[:, 0:HV * NH].rearrange("p (h k) -> p h k", h=HV),
                                    ALU.pow).then_inc(s_rh, 1)
                gather(0, *earlier(0, u, b, -2))
                scatter(0, *earlier(0, u, b, 3))
            steps(pool, step1, 0, 3, head=2)

            for c in range(4):
                pool.wait_ge(s_veps[1], c + 1)
                norms(0, quarter(c), s_rstd[1])
            pool.wait_ge(s_used, 2)
            paired(g)
            for b in range(3):
                gather(1, 0, b)

            def step2(u, b):
                gather(1, *earlier(1, u, b, -3))
                scatter(1, *earlier(1, u, b, 2))
            steps(pool, step2, 1, 2)

        @block.scalar
        def _(act):
            a = nc.scalar
            r = E * CH
            for m, w in enumerate((q_w, k_w, v_w)):
                act.dma_start(raw1[m * r:(m + 1) * r, :], w.rearrange("e (c n) o b -> (e c) (n o b)", c=CH)).then_inc(s_raw, 16)
            act.dma_start(raw1[3 * r:4 * r, :], conv_w.rearrange("e (c p) k -> (e c) (p k)", c=CH)).then_inc(s_raw, 16)
            act.dma_start(raw2, ig_w.rearrange("e (s p) h -> (e s) (p h)", p=P)).then_inc(s_raw, 16)

            def normed(l, src, c):
                act.wait_ge(s_rstd[l], c + 1)
                if l == 0:
                    act.wait_ge(s_x[c], 16)
                for i in range(c * TT // 4, (c + 1) * TT // 4):
                    ins = a.activation(x1[:, i, :], src[:, i, :], ACT.Identity, bias=shift[:, 0, i:i + 1], scale=rstd[:, 0, i:i + 1])
                ins.then_inc(s_x1[l], 1)

            def transposed(l, q):
                act.wait_ge(s_x1T[l], q + 1)
                a.activation(x1T[:, quarter(q), :].rearrange("p i t -> p (i t)"), bank[5 + q % 2][:, :],
                             ACT.Copy).then_inc(s_x1Tc[l], 1)

            normed(0, x, 0)
            normed(0, x, 1)
            act.wait_ge(s_parp, 1)
            a.activation(qkvT[:].rearrange("p b m -> p (b m)"), bank[0][:, 0:4 * 64], ACT.Copy)
            a.activation(igT[:].rearrange("p h m -> p (h m)"), bank[1][:, 0:4 * 48], ACT.Copy)
            a.activation(parT[:], bank[2][:, 0:64], ACT.Copy).then_inc(s_parT, 1)
            transposed(0, 0)
            for c in range(2, 4):
                normed(0, x, c)
                transposed(0, c - 1)
            transposed(0, 3)
            act.wait_ge(s_parT, 1)
            act.wait_ge(s_ib, 16)
            for m, (col, scale) in enumerate(((CB, 1.0), (ON, 1.0), (SK, 0.5))):
                a.activation(rec[:, :, col:col + CH], parT[:, m * r:(m + 1) * r].rearrange("p (e c) -> p e c", c=CH),
                             ACT.Copy, scale=scale).then_inc(s_par2, 1)

            def prepare1(e):
                p = e % 2
                act.wait_ge(s_pT, e + 1)
                if e >= 2:
                    act.wait_ge(s_pWv, e - 1)
                a.activation(mT[:, p].rearrange("p c t -> p (c t)"), bank[0][:, 0:I], ACT.Copy)
                for c in range(CH):
                    at = 3 * r + e * CH + c
                    a.activation(mTs[:, p, c, :], bank[0][:, c * P:(c + 1) * P], ACT.Copy,
                                 scale=qkvT[:, 3, at:at + 1]).then_inc(s_mT, 1)
                act.wait_ge(s_pV, e + 1)
                a.activation(vT[:, p].rearrange("p c t -> p (c t)"), bank[1][:, 0:CH * (P + NH)], ACT.Copy).then_inc(s_vT, 1)
                act.wait_ge(s_pKQ, e + 1)
                kq = bank[2][:, 0:CH * (P + NH)].rearrange("p (c n) -> p c n", c=CH)
                a.activation(rec[:, e, KQ:KQ + I].rearrange("p (c n) -> p c n", c=CH), kq[:, :, 0:P], ACT.Copy).then_inc(s_kq, 1)
                a.activation(rec[:, e, GC:GC + CH * NH].rearrange("p (c h) -> p c h", c=CH), kq[:, :, P:], ACT.Copy, scale=0.5).then_inc(s_kq, 1)

            def prepare2(e):
                act.wait_ge(s_pWc, e + 1)
                a.activation(rec[:, e, WC:WC + I], bank[3][:, 0:I], ACT.Copy).then_inc(s_wc, 1)
                act.wait_ge(s_pWv, e + 1)
                a.activation(rec[:, e, WV:WV + I].rearrange("p (c n) -> p c n", c=CH),
                             bank[4][:, 0:CH * (P + NH)].rearrange("p (c n) -> p c n", c=CH)[:, :, 0:P], ACT.Copy)
                a.activation(rec[:, e, GX:GX + NH], bank[4][:, P:P + NH], ACT.Copy).then_inc(s_rec, 1)

            for e in range(E):
                prepare1(e)
                if e:
                    prepare2(e - 1)
                if 2 <= e < 6:
                    act.wait_ge(s_rstdn, 1)
                    for i in range(TT // 2 + 2 * (e - 2), TT // 2 + 2 * (e - 1)):
                        ins = a.activation(xn[:, i, :], x[:, i, :], ACT.Identity, bias=shift[:, 1, i:i + 1], scale=rstd[:, 1, i:i + 1])
                if e == 5:
                    ins.then_inc(s_xn, 1)
                if e == 3:
                    act.wait_ge(s_top[0], 1)
                    a.activation(ex[:, :, 0], den[:, :, 0], ACT.Exp).then_inc(s_ex[0], 1)
            prepare2(E - 1)

            def index(l, u, b, dst, src, done):
                if active(l, u, b):
                    n = LTS[l] // P
                    a.activation(dst[:, b * n:(b + 1) * n], src[l][:, bass.ds(act.snap(n * (WAYS[l] * u + b)), n)],
                                 ACT.Copy).then_inc(done[l], 1)

            def in_copy1(u, b):
                if not active(0, u, b):
                    return
                j = 2 * u + b
                act.wait_ge(s_xtp[0], j + 1)
                at_least(act, s_z, j - 1)
                a.activation(xT[:, b, :], XT[:, 0:TS], ACT.Copy).then_inc(s_xts[0], 1)
                index(0, *earlier(0, u, b, -2), gi2, gidx, s_gi)

            def step1(u, b):
                j = 2 * u + b
                up, k1, k2 = active(0, u, b), active(0, u, b, 1), active(0, u, b, 2)
                if k1:
                    act.wait_ge(s_nig, j)
                    a.activation(eig[:], nig[:], ACT.Exp).then_inc(s_eig, 1)
                if up:
                    act.wait_ge(s_pc, j + 1)
                    act.wait_ge(s_wbuf[0][b], 16 * (u + 1))
                    at_least(act, s_ca, CH * (j - 1))
                    for c in range(CH):
                        a.activation(pre[:, b, c, :], PC[:, c * TS:(c + 1) * TS], ACT.Identity,
                                     bias=rbuf[:, b, CB + c:CB + c + 1]).then_inc(s_pre, 1)
                    act.wait_ge(s_pre, 2 * j + 2)
                    a.activation(thc[:, b], pre[:, b], ACT.Tanh, scale=0.5).then_inc(s_thc, 1)
                if up:
                    act.wait_ge(s_vc, j + 1)
                    at_least(act, s_c2v, j - 1)
                    for h in range(HV):
                        for k in range(NH):
                            o = h * I + k * DH
                            ins = a.activation(sq[:, h, k * DH:(k + 1) * DH], VC[b][:, o:o + DH], ACT.Square, scale=DH ** -0.5,
                                               accum_out=var[:, b, h, k:k + 1])
                    ins.then_inc(s_var, 1)
                    in_copy1(*earlier(0, u, b, -1))
                    act.wait_ge(s_ca, CH * (j + 1))
                    at_least(act, s_h1, j - 1)
                    for c in range(CH):
                        ins = a.activation(cask[:, b, c, :], ca[:, b, c, :], ACT.Copy,
                                           scale=rbuf[:, b, SK + c:SK + c + 1])
                    ins.then_inc(s_cask, 1)
                    act.wait_ge(s_z, j + 1)
                    at_least(act, s_zz, j - 1)
                    a.activation(thz[:, b], Z[:].rearrange("p (c t) -> p c t", c=CH), ACT.Tanh, scale=0.5).then_inc(s_thz, 1)
                if k2:
                    k, kb = earlier(0, u, b, 2)
                    y_out(0, k, kb, yb[:, kb], Y[:, 0:TS].rearrange("p (h d) -> p h d", h=HV))

            def y_out(l, k, kb, dst, src):
                act.wait_ge(s_y[l], WAYS[l] * k + kb + 1)
                at_least(act, s_scat[l][kb], 16 * (LTS[l] // P) * k)
                index(l, k, kb, si2, sidx, s_si)
                a.activation(dst, src, ACT.Copy).then_inc(s_yb[l], 1)
            in_copy1(0, 0)
            steps(act, step1, 0, 2, head=2)

            for c in range(4):
                normed(1, xres, c)
                transposed(1, c)
            act.wait_ge(s_top[1], 1)
            a.activation(ex[:], den[:], ACT.Exp, scale=-1.0).then_inc(s_ex[1], 1)

            def in_copy2(u, b):
                if active(1, u, b):
                    act.wait_ge(s_xtp[1], 4 * u + b + 1)
                    a.activation(xT2[:, b, :], bank[b % 2][:, 0:P], ACT.Copy).then_inc(s_xts[1], 1)

            def step2(u, b):
                j = 4 * u + b
                if active(1, u, b):
                    in_copy2(*earlier(1, u, b, -1))
                    index(1, *earlier(1, u, b, -3), gi2, gidx, s_gi)
                    act.wait_ge(s_g, j + 1)
                    at_least(act, s_gg, j - 3)
                    a.activation(th2[:, b], bank[4 + b][:, 0:I].rearrange("p (c t) -> p c t", c=CH), ACT.Tanh, scale=0.5)\
                        .then_inc(s_thg, 1)
                if active(1, u, b, 1):
                    k, kb = earlier(1, u, b, 1)
                    y_out(1, k, kb, yb2[:, kb, :], bank[2 + kb % 2][:, 0:D])
            in_copy2(0, 0)
            steps(act, step2, 1, 1, head=2)

        @block.tensor
        def _(pe):
            t = nc.tensor
            r = E * CH
            pe.wait_ge(s_pool, 2)

            def route_transposes(l, q):
                pe.wait_ge(s_x1[l], q + 1)
                if q >= 2:
                    pe.wait_ge(s_x1Tc[l], q - 1)
                for i in range(4):
                    ins = t.transpose(bank[5 + q % 2][:, i * P:(i + 1) * P], x1[:, 4 * q + i, :], ident[:])
                ins.then_inc(s_x1T[l], 1)

            def route_logits(l, q, w):
                pe.wait_ge(s_x1Tc[l], q + 1)
                for i in range(4 * q, 4 * q + 4):
                    ins = t.matmul(Lp[:, i * E:(i + 1) * E], x1T[:, i, :], w, start=True, stop=True)
                ins.then_inc(s_lg[l], 1)

            def param_transposes():
                pe.wait_ge(s_raw, 16 * 10)
                for b in range(QB):
                    t.transpose(bank[0][:, b * 64:(b + 1) * 64], raw1[:, b:4 * P:4], ident[0:64, 0:64])
                for h in range(NH):
                    t.transpose(bank[1][:, h * 48:(h + 1) * 48], raw2[:, h:4 * P:4], ident[0:48, 0:48])
                t.transpose(bank[2][:, 0:64], raw3[:], ident[0:64, 0:64]).then_inc(s_parp, 1)

            def route_rank(l):
                pe.wait_ge(s_picked[l], 1)
                pe.wait_ge(s_const, 1)
                pk = picked[:].rearrange("p i e -> p (i e)")
                t.matmul(Rp, lower[:], pk, start=True, stop=False, skip_group_check=True)
                for i in range(TT):
                    n = TT - i
                    ins = t.matmul(Rp[:, (i + 1) * E:].rearrange("p (n e) -> p n e", e=E), ones[:],
                                   picked[:, i:i + 1, :].to_broadcast([P, n, E]), start=False, stop=(i == TT - 1),
                                   skip_group_check=True)
                ins.then_inc(s_rank[l], 1)

            def route_perm(l):
                n = TT * TOPK
                pe.wait_ge(s_paired, l + 1)
                for c in range(n):
                    if c % 8 == 0:
                        pe.wait_ge(s_hot[l], c // 8 + 1)
                    ins = t.matmul(Mp, onehot[:, c, :], rhs[:, c, :], start=(c == 0), stop=(c == n - 1))
                ins.then_inc(s_perm[l], 1)

            def prepare1(e):
                pe.wait_ge(s_wl, e + 1)
                if e:
                    pe.wait_ge(s_mT, 2 * e)
                for c in range(CH):
                    ins = t.transpose(bank[0][:, c * P:(c + 1) * P], wraw[:, e, c * P:(c + 1) * P], ident[:])
                ins.then_inc(s_pT, 1)
                if e == 0:
                    pe.wait_ge(s_blk[0], 2)
                    pe.wait_ge(s_blk[1], 1)
                    pe.wait_ge(s_blk[2], 1)
                else:
                    pe.wait_ge(s_vT, e)
                pe.wait_ge(s_cig, e + 1)
                for c in range(CH):
                    o = c * (P + NH)
                    ins = t.matmul(bank[1][:, o:o + P + NH], blocks[:, 2 * r + e * CH + c, 0:P], cig[:, e % 2, c, :], start=True, stop=True)
                ins.then_inc(s_pV, 1)
                if e:
                    pe.wait_ge(s_kq, 2 * e)
                for c in range(CH):
                    o = c * (P + NH)
                    q, k = blocks[:, e * CH + c], blocks[:, r + e * CH + c]
                    t.matmul(bank[2][:, o:o + P + NH], k[:, 0:P], q, start=True, stop=False, skip_group_check=True)
                    ins = t.matmul(bank[2][:, o + P:o + P + NH], q[:, 0:P], igT[:, :, 6 * e + c], start=False, stop=True,
                                   skip_group_check=True)
                ins.then_inc(s_pKQ, 1)

            def prepare2(e):
                p = e % 2
                pe.wait_ge(s_mT, 2 * e + 2)
                if e:
                    pe.wait_ge(s_wc, e)
                for c in range(CH):
                    ins = t.transpose(bank[3][:, c * P:(c + 1) * P], mTs[:, p, c, :], ident[:])
                ins.then_inc(s_pWc, 1)
                pe.wait_ge(s_vT, e + 1)
                if e:
                    pe.wait_ge(s_rec, e)
                for c in range(CH):
                    ins = t.matmul(bank[4][:, c * P:(c + 1) * P + NH], mT[:, p, c, :], vT[:, p, c, :], start=(c == 0),
                                   stop=(c == CH - 1), skip_group_check=True)
                ins.then_inc(s_pWv, 1)

            route_transposes(0, 0)
            pe.wait_ge(s_gate, 16)
            param_transposes()
            for q in range(1, 4):
                route_transposes(0, q)
                route_logits(0, q - 1, gate[:])
            route_logits(0, 3, gate[:])
            pe.wait_ge(s_parT, 1)
            prepare1(0)
            prepare1(1)
            route_rank(0)
            prepare2(0)
            for e in range(2, 7):
                prepare1(e)
                prepare2(e - 1)
            route_perm(0)
            for e in range(7, E):
                prepare1(e)
                prepare2(e - 1)
            prepare2(E - 1)
            pe.wait_ge(s_rec, E)
            pe.wait_ge(s_idx[0], 1)
            pe.wait_ge(s_late, 80)

            def in_transposes(l, u, b, dst):
                n = LTS[l] // P
                pe.wait_ge(s_gath[l][b], 16 * n * (u + 1))
                for h in range(n):
                    ins = t.transpose(dst[:, h * P:(h + 1) * P], xg2[:, b * n + h, :], ident[:])
                ins.then_inc(s_xtp[l], 1)

            def down(k, kb, l, dst):
                for h in range(LTS[l] // P):
                    for c in range(CH):
                        if l:
                            lhsT, rhs_ = hh2[:, kb, c, :], r2buf[:, kb, DOWN + c * D:DOWN + (c + 1) * D]
                        else:
                            lhsT, rhs_ = hs[:, kb, c, h * P:(h + 1) * P], wdbuf[:, kb, c, :]
                        ins = t.matmul(dst[:, h * D:(h + 1) * D], lhsT, rhs_, start=(c == 0), stop=(c == CH - 1))
                ins.then_inc(s_y[l], 1)

            def step1(u, b):
                j = 2 * u + b
                up, k1, k2 = active(0, u, b), active(0, u, b, 1), active(0, u, b, 2)

                def project(dst, col, src, c):
                    return t.matmul(dst[:, c * TS:(c + 1) * TS], rbuf[:, b, col + c * P:col + (c + 1) * P], src,
                                    start=True, stop=True)

                if up:
                    pe.wait_ge(s_xts[0], j + 1)
                    pe.wait_ge(s_wbuf[0][b], 16 * (u + 1))
                    at_least(pe, s_pre, 2 * j)
                    for c in range(CH):
                        ins = project(PC, WC, xT[:, b, :], c)
                    ins.then_inc(s_pc, 1)
                if k2:
                    pe.wait_ge(s_vs, j - 1)
                    at_least(pe, s_h1, j - 2)
                    for c in range(CH):
                        for h in range(HV):
                            o = c * TS + h * P
                            ins = t.transpose(VT[:, o:o + P], vs[:, h, c * P:(c + 1) * P], ident[:])
                    ins.then_inc(s_vt, 1)
                if up:
                    at_least(pe, s_vs, j - 1)
                    at_least(pe, s_stf, j)
                    for h in range(HV):
                        tok = slice(h * P, (h + 1) * P)
                        ins = t.matmul(VC[b][:, h * I:(h + 1) * I], xT[:, b, tok], rbuf[:, b, WV:WV + I], start=True, stop=True)
                        t.matmul(ig[:, h, :], xT[:, b, tok], rbuf[:, b, GX:GX + NH], start=(h == 0), stop=False,
                                 skip_group_check=True)
                    ins.then_inc(s_vc, 1)
                    v, vb = earlier(0, u, b, -1)
                    if active(0, v, vb):
                        at_least(pe, s_h1, j - 1)
                        in_transposes(0, v, vb, XT)
                    at_least(pe, s_zz, j)
                    for c in range(CH):
                        ins = project(Z, WZ, xT[:, b, :], c)
                    ins.then_inc(s_z, 1)
                    at_least(pe, s_prod, j)
                    for c in range(CH):
                        pe.wait_ge(s_ca, CH * j + c + 1)
                        ins = project(A, KQ, ca[:, b, c, :], c)
                    ins.then_inc(s_a, 1)
                    for h in range(HV):
                        for c in range(CH):
                            ins = t.matmul(ig[:, h, :], ca[:, b, c, h * P:(h + 1) * P], rbuf[:, b, GC + c * NH:GC + (c + 1) * NH],
                                           start=False, stop=(c == CH - 1), skip_group_check=True)
                    ins.then_inc(s_ig, 1)
                if k2:
                    k, kb = earlier(0, u, b, 2)
                    pe.wait_ge(s_wdbuf[kb], 16 * (k + 1))
                    pe.wait_ge(s_hs, 2 * k + kb + 1)
                    at_least(pe, s_yb[0], 2 * k + kb)
                    down(k, kb, 0, Y)
                if up:
                    pe.wait_ge(s_prod, j + 1)
                    for h in range(HV):
                        for c in range(CH):
                            ins = t.matmul(qk[:, h, :], prod[:, b, c, h * P:(h + 1) * P], headsum[:, c, :],
                                           start=False, stop=(c == CH - 1), skip_group_check=True)
                    ins.then_inc(s_st, 1)
            in_transposes(0, 0, 0, XT)
            steps(pe, step1, 0, 2, head=2)

            router = parT[:, 3 * r + E:3 * r + 2 * E]
            for q in range(4):
                route_transposes(1, q)
                route_logits(1, q, router)
            route_rank(1)
            route_perm(1)
            pe.wait_ge(s_idx[1], 1)

            def step2(u, b):
                j = 4 * u + b
                if active(1, u, b):
                    v, vb = earlier(1, u, b, -1)
                    if active(1, v, vb):
                        in_transposes(1, v, vb, bank[vb % 2])
                    pe.wait_ge(s_xts[1], j + 1)
                    pe.wait_ge(s_wbuf[1][b], 16 * (u + 1))
                    at_least(pe, s_hh, j - 3)
                    for col in (GATE, UP):
                        for c in range(CH):
                            o = col + c * P
                            ins = t.matmul(bank[4 + b][:, o:o + P], r2buf[:, b, o:o + P], xT2[:, b, :], start=True, stop=True)
                    ins.then_inc(s_g, 1)
                if active(1, u, b, 1):
                    k, kb = earlier(1, u, b, 1)
                    pe.wait_ge(s_hh, 4 * k + kb + 1)
                    at_least(pe, s_yb[1], 4 * k + kb - 1)
                    down(k, kb, 1, bank[2 + kb % 2])
            in_transposes(1, 0, 0, bank[0])
            steps(pe, step2, 1, 1)

        @block.vector
        def _(dve):
            v = nc.vector
            count = [0]

            def done(ins):
                count[0] += 1
                ins.then_inc(s_dve, 1)
                dve.wait_ge(s_dve, count[0])

            def wide(ap, shape):
                return ap.to_broadcast(shape)

            def stats(src, cols):
                for i in cols:
                    ins = v.bn_stats(bn[:, i, :], src[:, i, :])
                done(ins)
                for i in cols:
                    ins = v.bn_aggr(mv[:, i, :], bn[:, i, :])
                return ins

            def route(l):
                dve.wait_ge(s_lg[l], 4)
                done(v.tensor_copy(lg[:], Lp.rearrange("p (i e) -> p i e", e=E)))
                row = [P, TT, E]
                for k in range(TOPK):
                    done(v.tensor_reduce(top[:, :, k], lg[:], AXX, ALU.max))
                    done(v.tensor_tensor(key[:], lg[:], wide(top[:, :, k:k + 1], row), ALU.is_equal))
                    done(v.tensor_tensor(key[:], key[:], wide(ekey[:].unsqueeze(1), row), ALU.mult))
                    done(v.tensor_reduce(kmax[:], key[:], AXX, ALU.max))
                    done(v.tensor_tensor(pick[:, :, k, :], key[:], wide(kmax[:].unsqueeze(2), row), ALU.is_equal))
                    if k == 0:
                        done(v.scalar_tensor_tensor(lg[:], pick[:, :, 0, :], -1e30, lg[:], ALU.mult, ALU.add))
                v.tensor_tensor(picked[:, 0:TT, :], pick[:, :, 0, :], pick[:, :, 1, :], ALU.add).then_inc(s_picked[l], 1)
                if l == 0:
                    v.tensor_tensor(den[:, :, 0], top[:, :, 1], top[:, :, 0], ALU.subtract).then_inc(s_top[0], 1)
                else:
                    v.tensor_scalar(den[:], top[:], -EXP_MAX, None, ALU.max).then_inc(s_top[1], 1)
                if l == 0:
                    for e in range(E // 2, E):
                        fold_z(e)
                dve.wait_ge(s_rank[l], 1)
                cuts = tilecut[:, 0:NTOK // P:LTS[l] // P]
                sqn, sq8 = [P, E, NTOK // LTS[l]], [P, E, E]
                over = cmpn[:, :, 0:NTOK // LTS[l]]
                done(v.tensor_tensor(over, wide(Rp[:, TT * E:].unsqueeze(2), sqn), wide(cuts.unsqueeze(1), sqn), ALU.is_gt))
                done(v.tensor_reduce(ntile[:], over, AXX, ALU.add))
                done(v.tensor_tensor(cmp8[:], wide(ntile[:].unsqueeze(1), sq8), upto[:], ALU.mult))
                done(v.tensor_reduce(cum[:], cmp8[:], AXX, ALU.add))
                done(v.tensor_tensor(before[:], cum[:], ntile[:], ALU.subtract))
                done(v.scalar_tensor_tensor(place[:], wide(before[:].unsqueeze(1), row), float(LTS[l]),
                                            Rp[:, 0:TT * E].rearrange("p (i e) -> p i e", e=E), ALU.mult, ALU.add))
                done(v.tensor_tensor(pslot[:], pick[:], wide(place[:].unsqueeze(2), [P, TT, TOPK, E]), ALU.mult))
                done(v.tensor_reduce(slot[:].rearrange("p (i k) -> p i k", k=TOPK), pslot[:], AXX, ALU.add))
                done(v.tensor_copy(sloti[:], slot[:]))
                v.tensor_scalar(loi[:], sloti[:], P - 1, None, ALU.bitwise_and)
                done(v.tensor_scalar(hii[:], sloti[:], 7, None, ALU.logical_shift_right))
                v.tensor_copy(lof[:], loi[:])
                done(v.tensor_copy(hif[:], hii[:]))
                n = TT * TOPK
                used = rhs[:, :, 2 * NA:3 * NA]
                v.tensor_tensor(used, wide(hif[:].unsqueeze(2), [P, n, NA]), wide(iota_a[:].unsqueeze(1), [P, n, NA]), ALU.is_equal)\
                    .then_inc(s_used, 1)
                dve.wait_ge(s_used, l + 1)
                if l == 0:
                    paired(v)
                v.tensor_scalar(rhs[:, :, 0:NA], used, part[:, 0:1], None, ALU.mult)
                for c in range(n):
                    ins = v.tensor_scalar(onehot[:, c, :], iota_p[:], lof[:, c:c + 1], None, ALU.is_equal)
                    if c % 8 == 7:
                        ins.then_inc(s_hot[l], 1)
                n = LNT[l] + 1
                jrow = [1, n, E]
                done(v.tensor_tensor(cmpj[:, 0:n], wide(cum[0:1, :].unsqueeze(1), jrow), wide(tileno[0:1, 0:n].unsqueeze(2), jrow), ALU.is_le))
                done(v.tensor_reduce(ej[:, 0:n], cmpj[:, 0:n], AXX, ALU.add))
                v.tensor_scalar(expert[l][:], ej[:, 0:n], float(E - 1), None, ALU.min).then_inc(s_exp[l], 1)
                dve.wait_ge(s_perm[l], 1)
                done(v.tensor_copy(perm[:], Mp))
                done(v.scalar_tensor_tensor(pairf[:], perm[:, 0:NA], float(TOPK * TT), perm[:, NA:2 * NA], ALU.mult, ALU.add))
                v.tensor_tensor(unused[:], perm[:, 2 * NA:3 * NA], spare[:], ALU.mult)
                done(v.tensor_copy(pairi[:], pairf[:]))
                v.tensor_scalar(gidx[l][:], pairi[:], 1, None, ALU.logical_shift_right)
                first = 2 + l
                n = first * LTS[l] // P
                v.tensor_scalar(gi2[:, 0:n], pairi[:, 0:n], 1, None, ALU.logical_shift_right).then_inc(s_gi[l], first)
                done(v.tensor_tensor(unused[:], spare[:], unused[:], ALU.subtract))
                v.tensor_tensor(sidx[l][:], pairf[:], unused[:], ALU.add).then_inc(s_idx[l], 1)
                dve.wait_ge(s_ex[l], 1)
                if l == 0:
                    done(v.tensor_scalar(den[:, :, 1], ex[:, :, 0], 1.0, None, ALU.add))
                    done(v.reciprocal(wt[:, :, 0], den[:, :, 1]))
                    done(v.tensor_tensor(wt[:, :, 1], ex[:, :, 0], wt[:, :, 0], ALU.mult))
                    v.tensor_tensor(wsum[:], wt[:, :, 0], wt[:, :, 1], ALU.add)
                    done(v.tensor_scalar(wh[0][:], wt[:], 0.5, None, ALU.mult))
                else:
                    done(v.tensor_scalar(den[:], ex[:], 1.0, None, ALU.add))
                    done(v.reciprocal(wt[:], den[:]))
                    done(v.tensor_tensor(wsum[:], wt[:, :, 0], wt[:, :, 1], ALU.add))
                    done(v.tensor_scalar(wsum[:], wsum[:], 1e-10, None, ALU.add))
                    done(v.reciprocal(kmax[:], wsum[:]))
                    done(v.scalar_tensor_tensor(wh[1][:], wt[:], 0.5, wide(kmax[:].unsqueeze(2), [P, TT, TOPK]), ALU.mult, ALU.mult))

            def moments(l, src, c):
                done(stats(src, range(c * TT // 4, (c + 1) * TT // 4)))
                v.tensor_scalar(veps[:, 0, quarter(c)], mv[:, quarter(c), 1], EPS, None, ALU.add)
                v.tensor_scalar(nmean[:, quarter(c)], mv[:, quarter(c), 0], -1.0, None, ALU.mult).then_inc(s_veps[l], 1)

            for c in range(4):
                dve.wait_ge(s_x[c], 16)
                moments(0, x, c)
            dve.wait_ge(s_veps[0], 4)
            v.scalar_tensor_tensor(veps[:, 1, :], veps[:, 0, :], EPS, mv[:, :, 1], ALU.mult, ALU.add).then_inc(s_vepsn, 1)
            dve.wait_ge(s_parT, 1)
            for m in (2, 0, 1):
                spread_blocks(m)

            def fold_z(e):
                at = 3 * E * CH + e
                v.tensor_scalar(rec[:, e, WZ:WZ + I], wraw[:, e, I:2 * I], parT[:, at:at + 1], None, ALU.mult).then_inc(s_wz, 1)

            dve.wait_ge(s_wraw, 16)
            for e in range(E // 2):
                fold_z(e)
            dve.wait_ge(s_const, 1)
            route(0)
            dve.wait_ge(s_xn, 2)
            for i in range(TT):
                ins = v.scalar_tensor_tensor(xres[:, i, :], x1[:, i, :], wsum[:, i:i + 1], x[:, i, :], ALU.mult, ALU.add)
            done(ins)

            K = 7

            def step1(u, b):
                j = 2 * u + b
                up, k1, k2 = active(0, u, b), active(0, u, b, 1), active(0, u, b, 2)
                kb = earlier(0, u, b, 1)[1]
                base = K * (j - 1)

                if k1:
                    dve.wait_ge(s_st, j)
                    dve.wait_ge(s_onib, j)
                    v.scalar_tensor_tensor(nig0[:], ig, -1.0, onib[:, kb, CH:].unsqueeze(1).to_broadcast([P, HV, NH]),
                                           ALU.mult, ALU.subtract).then_inc(s_cell, 1)
                    v.tensor_copy(qks[:], qk).then_inc(s_stf, 1)
                    dve.wait_ge(s_cell, base + 1)
                    at_least(dve, s_eig, j - 1)
                    v.tensor_scalar(nig[:], nig0[:], EXP_MAX, None, ALU.min).then_inc(s_nig, 1)
                    dve.wait_ge(s_stf, j)
                    v.scalar_tensor_tensor(absqk[:], qks[:], -1.0, qks[:], ALU.mult, ALU.max).then_inc(s_cell, 1)
                if k1:
                    dve.wait_ge(s_thz, j)
                    v.scalar_tensor_tensor(zz[:, kb], thz[:, kb], 1.0, Z[:].rearrange("p (c t) -> p c t", c=CH), ALU.add, ALU.mult).then_inc(s_zz, 1)
                    dve.wait_ge(s_cell, base + 2)
                    v.tensor_scalar(abs6[:], absqk[:], CELL_EPS, None, ALU.add).then_inc(s_cell, 1)
                    dve.wait_ge(s_cell, base + 3)
                    dve.wait_ge(s_eig, j)
                    v.scalar_tensor_tensor(nrm6[:], eig[:], CELL_EPS, abs6[:], ALU.add, ALU.max).then_inc(s_cell, 1)
                if k2:
                    dve.wait_ge(s_vt, j - 1)
                    dve.wait_ge(s_cask, j - 1)
                    h1_chunk(b, 0)
                if k1:
                    dve.wait_ge(s_cell, base + 4)
                    v.reciprocal(rn[:], nrm6[:]).then_inc(s_cell, 1)
                if k2:
                    h1_chunk(b, 1).then_inc(s_h1, 1)
                if k1:
                    dve.wait_ge(s_cell, base + 5)
                    v.tensor_tensor(cc[:], qks[:], rn[:], ALU.mult).then_inc(s_cell, 1)
                    dve.wait_ge(s_cell, base + 6)
                    v.tensor_tensor(c2[:], cc[:], cc[:], ALU.mult).then_inc(s_cell, 1)
                if up:
                    dve.wait_ge(s_thc, j + 1)
                    at_least(dve, s_st, j - 1)
                    at_least(dve, s_cask, j - 1)
                    ca_chunk(b, 0)
                if k1:
                    dve.wait_ge(s_cell, base + 7)
                    dve.wait_ge(s_var, j)
                    at_least(dve, s_rh, j - 1)
                    v.tensor_tensor(c2v[:], var[:, kb], c2[:], ALU.mult).then_inc(s_c2v, 1)
                if up:
                    ca_chunk(b, 1)
                if k1:
                    dve.wait_ge(s_c2v, j)
                    v.tensor_scalar(c2ve[:], c2v[:], EPS, None, ALU.add).then_inc(s_c2ve, 1)
                if k2:
                    dve.wait_ge(s_h1, j - 1)
                    v.tensor_tensor(hs[:, b], h1[:], zz[:, b], ALU.mult).then_inc(s_hs, 1)
                if up:
                    dve.wait_ge(s_wbuf[0][b], 16 * (u + 1))
                    v.tensor_copy(onib[:, b], rbuf[:, b, ON:ON + CH + NH]).then_inc(s_onib, 1)
                    dve.wait_ge(s_a, j + 1)
                    v.tensor_tensor(prod[:, b], A[:].rearrange("p (c t) -> p c t", c=CH), ca[:, b], ALU.mult).then_inc(s_prod, 1)
                if k1:
                    dve.wait_ge(s_rh, j)
                    v.tensor_tensor(ss[:].rearrange("p (h k) -> p h k", h=HV), cc[:], rh[:], ALU.mult).then_inc(s_ss, 1)
                    dve.wait_ge(s_ss, j)
                    at_least(dve, s_vt, j - 1)
                    v.tensor_tensor(vs[:].rearrange("p h (k d) -> p (h k) d", d=DH), VC[kb][:].rearrange("p (k d) -> p k d", d=DH),
                                    ss[:].unsqueeze(2).to_broadcast([P, HV * NH, DH]), ALU.mult).then_inc(s_vs, 1)

            def ca_chunk(b, c):
                return v.scalar_tensor_tensor(ca[:, b, c], thc[:, b, c], 1.0, pre[:, b, c], ALU.add, ALU.mult).then_inc(s_ca, 1)

            def h1_chunk(b, c):
                return v.scalar_tensor_tensor(h1[:, c, :], VT[:, c * TS:(c + 1) * TS], onib[:, b, c:c + 1],
                                              cask[:, b, c, :], ALU.mult, ALU.add)
            steps(dve, step1, 0, 2)

            def combine(l, c):
                cols = range(c * TT // 4, (c + 1) * TT // 4)
                dve.wait_ge(s_yin[l][c], 16)
                for k in range(TOPK):
                    for i in cols:
                        ins = v.scalar_tensor_tensor(xres[:, i, :], ypair[:, TOPK * i + k, :], wh[l][:, i, k:k + 1], xres[:, i, :], ALU.mult, ALU.add)
                    if k == 0:
                        done(ins)
                return ins, cols

            for c in range(4):
                done(combine(0, c)[0])
                moments(1, xres, c)
            route(1)

            def step2(u, b):
                if not active(1, u, b):
                    return
                j = 4 * u + b
                both = bank[4 + b][:].rearrange("p (g c t) -> p g c t", g=2, c=CH)
                dve.wait_ge(s_thg, j + 1)
                v.scalar_tensor_tensor(gg2[:, b], th2[:, b], 1.0, both[:, 0], ALU.add, ALU.mult).then_inc(s_gg, 1)
                dve.wait_ge(s_gg, j + 1)
                at_least(dve, s_y[1], j - 3)
                v.tensor_tensor(hh2[:, b], both[:, 1], gg2[:, b], ALU.mult).then_inc(s_hh, 1)
            steps(dve, step2, 1, 0)
            for c in range(4):
                combine(1, c)[0].then_inc(s_out, 1)


_INS = ["hidden_states", "gate_w", "ln_w", "w_up", "conv_w", "conv_b", "q_w", "k_w", "v_w", "ig_w", "ig_b",
        "on_w", "skip_w", "w_down"]
_FFN = ["router_w", "w_gate", "w_up", "w_down"]


def kernel(**inputs):
    import numpy as _np
    import concourse.bacc as _bacc
    from concourse import mybir as _mybir
    from concourse.bass_utils import run_bass_kernel_spmd as _run

    nc = _bacc.Bacc("TRN2", target_bir_lowering=False, num_devices=1)
    arrays, args = {}, []
    for name in ["L0_attn_" + n for n in _INS] + ["L0_ffn_" + n for n in _FFN]:
        a = _np.ascontiguousarray(inputs[name])
        arrays[f"in_{name}"] = a
        args.append(nc.dram_tensor(f"in_{name}", a.shape, _mybir.dt.from_np(a.dtype), kind="ExternalInput").ap())
    args.append(nc.dram_tensor("out_0", inputs["L0_attn_hidden_states"].shape, _mybir.dt.float32, kind="ExternalOutput").ap())
    program(nc, *args)
    return _run(nc, [arrays], core_ids=[0]).results[0]["out_0"]
```
